# Optimizing a Trainium2 kernel written in Bass

```python
import numpy as np
import jax
import jax.numpy as jnp

def _softmax(x, axis=-1):
    return jax.nn.softmax(x, axis=axis)

def _gelu(x):
    return jax.nn.gelu(x, approximate=True)

def _silu(x):
    return jax.nn.silu(x)

def _sigmoid(x):
    return jax.nn.sigmoid(x)

def _layernorm(x, axis=-1, eps=1e-05):
    m = jnp.mean(x, axis=axis, keepdims=True)
    v = jnp.var(x, axis=axis, keepdims=True)
    return (x - m) / jnp.sqrt(v + eps)

def _scatter_add(tgt, idx, src, axis=0):
    return tgt.at[idx].add(src)

def _segment_sum(src, seg, n):
    return jax.ops.segment_sum(src, seg, n)
kernel_name = 'mk_xattn_ffn_d1_seqx_r8_71bc03'

def setup_inputs(seed: int=0):
    np.random.seed(seed)
    _w = jnp.asarray

    def _rec_inputs():
        import jax
        import jax.numpy as jnp
        _rk = jax.random.key(seed)
        x = -0.0003929 + 0.9999 * jax.random.normal(jax.random.fold_in(_rk, 1), (16, 128, 128), jnp.float32)
        _lenS = 128 - jax.random.randint(jax.random.fold_in(_rk, 7), (16,), 0, max(1, 128 // 4) + 1, jnp.int32)
        _lenS2 = 128 - jax.random.randint(jax.random.fold_in(_rk, 8), (16,), 0, max(1, 128 // 4) + 1, jnp.int32)
        _ctx_1024P = jax.random.normal(jax.random.fold_in(_rk, 11), (16, 16, 128), jnp.float32)
        _ctx_1024c = jax.random.dirichlet(jax.random.fold_in(_rk, 511), 0.3 * jnp.ones((16,), jnp.float32), (16, 128))
        _ctx_1024t = jnp.einsum('bsk,bkd->bsd', _ctx_1024c, _ctx_1024P)
        _ctx_1024t = _ctx_1024t * jax.lax.rsqrt(jnp.mean(jnp.square(_ctx_1024t)) + 1e-12) * 0.953939
        ctx_1024 = 2.81802e-05 + 1.00001 * (_ctx_1024t + 0.3 * jax.random.normal(jax.random.fold_in(_rk, 611), (16, 128, 128), jnp.float32))
        return (x, ctx_1024)
    x, ctx_1024 = _rec_inputs()

    def _L0_xattn_setup():
        import jax, jax.numpy as jnp
        import numpy as np
        D_MODEL = 128
        H = 16
        HEAD_DIM = D_MODEL // H
        D_K = 64
        D_V = 64
        key = jax.random.key(seed)
        ks = jax.random.split(key, 11)
        B, L = (4, 512)
        s_in = 1.0 / np.sqrt(HEAD_DIM)
        s_out = 1.0 / np.sqrt(H * D_V)
        return {'Q': jax.random.normal(ks[0], (B, L, D_MODEL), jnp.float32), 'K': jax.random.normal(ks[1], (B, L, D_MODEL), jnp.float32), 'V': jax.random.normal(ks[2], (B, L, D_MODEL), jnp.float32), 'Wq': jax.random.normal(ks[3], (HEAD_DIM, D_K), jnp.float32) * s_in, 'bq': jnp.zeros((D_K,), jnp.float32), 'Wk': jax.random.normal(ks[4], (HEAD_DIM, D_K), jnp.float32) * s_in, 'bk': jnp.zeros((D_K,), jnp.float32), 'Wv': jax.random.normal(ks[5], (HEAD_DIM, D_V), jnp.float32) * s_in, 'bv': jnp.zeros((D_V,), jnp.float32), 'Wo': jax.random.normal(ks[6], (H * D_V, D_MODEL), jnp.float32) * s_out, 'bo': jnp.zeros((D_MODEL,), jnp.float32)}
    _L0_xattn_all = _L0_xattn_setup()
    _L0_xattn_in = {k: v for k, v in _L0_xattn_all.items() if k in ('Wq', 'bq', 'Wk', 'bk', 'Wv', 'bv', 'Wo', 'bo')}
    del _L0_xattn_all

    def _L0_ffn_setup():
        import jax, jax.numpy as jnp
        import numpy as np
        E = 8
        K = 2
        D = 128
        F = 512

        def _selected_matmul(inp, weight, scales, one_hot):
            wq = weight * scales
            all_out = jnp.einsum('mk,bkn->bmn', inp, wq)
            return jnp.einsum('bm,bmn->mn', one_hot, all_out)
        key = jax.random.key(seed)
        ks = jax.random.split(key, 8)
        inputs = jax.random.normal(ks[0], (1, 256, D), dtype=jnp.float32)
        router_w = jax.random.normal(ks[1], (D, E), dtype=jnp.float32) * 0.02
        wv = jax.random.normal(ks[2], (E, D, F), dtype=jnp.float32) * 0.02
        sv = jax.random.uniform(ks[3], (E, 1, F), dtype=jnp.float32, minval=0.5, maxval=1.5)
        w = jax.random.normal(ks[4], (E, D, F), dtype=jnp.float32) * 0.02
        s = jax.random.uniform(ks[5], (E, 1, F), dtype=jnp.float32, minval=0.5, maxval=1.5)
        w1 = jax.random.normal(ks[6], (E, F, D), dtype=jnp.float32) * 0.02
        s1 = jax.random.uniform(ks[7], (E, 1, D), dtype=jnp.float32, minval=0.5, maxval=1.5)
        return {'inputs': inputs, 'router_w': router_w, 'wv': wv, 'sv': sv, 'w': w, 's': s, 'w1': w1, 's1': s1}
    _L0_ffn_all = _L0_ffn_setup()
    _L0_ffn_in = {k: v for k, v in _L0_ffn_all.items() if k in ('router_w', 'wv', 'sv', 'w', 's', 'w1', 's1')}
    del _L0_ffn_all
    return {'x': x, 'ctx_1024': ctx_1024, 'L0_xattn_Wq': _L0_xattn_in['Wq'], 'L0_xattn_bq': _L0_xattn_in['bq'], 'L0_xattn_Wk': _L0_xattn_in['Wk'], 'L0_xattn_bk': _L0_xattn_in['bk'], 'L0_xattn_Wv': _L0_xattn_in['Wv'], 'L0_xattn_bv': _L0_xattn_in['bv'], 'L0_xattn_Wo': _L0_xattn_in['Wo'], 'L0_xattn_bo': _L0_xattn_in['bo'], 'L0_ffn_router_w': _L0_ffn_in['router_w'], 'L0_ffn_wv': _L0_ffn_in['wv'], 'L0_ffn_sv': _L0_ffn_in['sv'], 'L0_ffn_w': _L0_ffn_in['w'], 'L0_ffn_s': _L0_ffn_in['s'], 'L0_ffn_w1': _L0_ffn_in['w1'], 'L0_ffn_s1': _L0_ffn_in['s1']}

def reference(x, ctx_1024, L0_xattn_Wq, L0_xattn_bq, L0_xattn_Wk, L0_xattn_bk, L0_xattn_Wv, L0_xattn_bv, L0_xattn_Wo, L0_xattn_bo, L0_ffn_router_w, L0_ffn_wv, L0_ffn_sv, L0_ffn_w, L0_ffn_s, L0_ffn_w1, L0_ffn_s1):
    import jax
    import jax.numpy as jnp

    def _L0_xattn_ref(Q, K, V, Wq, bq, Wk, bk, Wv, bv, Wo, bo):
        import jax, jax.numpy as jnp
        import numpy as np
        D_MODEL = 128
        H = 16
        HEAD_DIM = D_MODEL // H
        D_K = 64
        D_V = 64
        B, L, D = Q.shape
        Qr = Q.reshape(B, L, H, HEAD_DIM)
        Kr = K.reshape(B, L, H, HEAD_DIM)
        Vr = V.reshape(B, L, H, HEAD_DIM)
        Q_ = Qr @ Wq + bq
        K_ = Kr @ Wk + bk
        V_ = Vr @ Wv + bv
        scores = jnp.einsum('blhk,blgk->blhg', Q_, K_) / jnp.sqrt(jnp.float32(D_K))
        attn = jax.nn.softmax(scores, axis=-1)
        x = jnp.einsum('blhg,blgv->blhv', attn, V_)
        x = x.reshape(B, L, H * D_V)
        return x @ Wo + bo

    def _L0_ffn_ref(inputs, router_w, wv, sv, w, s, w1, s1):
        import jax, jax.numpy as jnp
        import numpy as np
        E = 8
        K = 2
        D = 128
        F = 512

        def _selected_matmul(inp, weight, scales, one_hot):
            wq = weight * scales
            all_out = jnp.einsum('mk,bkn->bmn', inp, wq)
            return jnp.einsum('bm,bmn->mn', one_hot, all_out)
        B, S, Dm = inputs.shape
        x = inputs.reshape(B * S, Dm)
        logits = jnp.dot(x.astype(jnp.float32), router_w)
        probs = jax.nn.softmax(logits, axis=-1)
        expert_gate, expert_index = jax.lax.top_k(probs, K)
        xb = jnp.repeat(x, K, axis=0)
        one_hot = jax.nn.one_hot(expert_index.reshape(-1), E, axis=0)
        v = _selected_matmul(xb, wv, sv, one_hot)
        y = jax.nn.gelu(_selected_matmul(xb, w, s, one_hot))
        out = _selected_matmul(v * y, w1, s1, one_hot)
        out = out.reshape(B, S, K, Dm)
        out = jnp.sum(expert_gate.reshape(B, S, K, 1) * out, axis=2)
        return out
    x = x + _L0_xattn_ref(_layernorm(x, axis=-1), ctx_1024, ctx_1024, L0_xattn_Wq, L0_xattn_bq, L0_xattn_Wk, L0_xattn_bk, L0_xattn_Wv, L0_xattn_bv, L0_xattn_Wo, L0_xattn_bo)
    x = x + _L0_ffn_ref(_layernorm(x, axis=-1), L0_ffn_router_w, L0_ffn_wv, L0_ffn_sv, L0_ffn_w, L0_ffn_s, L0_ffn_w1, L0_ffn_s1)
    return x

_drawn_inputs = setup_inputs


def setup_inputs(seed=0):
    import zlib

    import numpy as np

    out = dict(_drawn_inputs(seed))
    spreads = {'L0_xattn_bq': (0.0, 0.1),
     'L0_xattn_bk': (0.0, 0.1),
     'L0_xattn_bv': (0.0, 0.1),
     'L0_xattn_bo': (0.0, 0.1)}
    factors = {}
    for name, (base, spread) in spreads.items():
        noise = np.random.default_rng([zlib.crc32(name.encode()), seed]).standard_normal(out[name].shape)
        drawn = base * np.exp(spread * noise) if base else spread * noise
        out[name] = jnp.asarray(drawn.astype(out[name].dtype))
    for name, factor in factors.items():
        out[name] = (out[name] * factor).astype(out[name].dtype)
    return out
```

```python
from contextlib import ExitStack

import concourse.bass as bass
from concourse import mybir

ALU = mybir.AluOpType
ACT = mybir.ActivationFunctionType
AX_X = mybir.AxisListType.X
F32 = mybir.dt.float32
I32 = mybir.dt.int32

P = 128
NT = 16
G = 4
NG = NT // G
H = 16
HD = 8
DK = 64
QW = (HD + 1) * H
E = 8
F = 512
FC = F // P
TOP = 2
ROWW = P + 2
TOKENS = NT * P
REGION = TOKENS + P
TILES = (TOP * TOKENS + E * (P - 1)) // P
SPARE = TOP * G
assert SPARE >= TILES - TOP * TOKENS // P
ROWS = E * REGION + SPARE * P
NOWHERE = 1 << 20
XB = 6
EPS = 1e-5
SCALE = DK ** -0.5


def xattn_moe_kernel(nc, x, ctx, Wq, bq, Wk, bk, Wv, bv, Wo, bo, router_w, wv, sv, w, s, w1, s1, out):
    stack = ExitStack()
    with stack:
        def sb(name, shape, dt=F32):
            return stack.enter_context(nc.sbuf_tensor(name, shape, dt))

        def sem(name):
            return stack.enter_context(nc.semaphore(name))

        bank = [stack.enter_context(nc.psum_tensor(f"bank{i}", [P, 512], F32)) for i in range(8)]

        routed = nc.dram_tensor("routed", [ROWS, ROWW], F32, kind="Internal").ap()
        expert_out = nc.dram_tensor("expert_out", [TOP * TOKENS, P], F32, kind="Internal").ap()

        ident = sb("ident", [P, P])
        ones = sb("ones", [P, P])
        before = sb("before", [P, P])
        head_mask = sb("head_mask", [P, H])
        minus_half = sb("minus_half", [P, NT])
        eps = sb("eps", [P, NT])
        pause_pool, pause_dve = sb("pause_pool", [P, 1]), sb("pause_dve", [P, 1])
        rev = sb("rev", [P, G, E])
        region0 = sb("region0", [P, G, E])
        tile_edges = sb("tile_edges", [P, E, NT])
        tile_no = sb("tile_no", [P, TILES, E])
        pad_rows = sb("pad_rows", [P, ROWW])

        q9 = sb("q9", [HD + 1, DK])
        k9 = sb("k9", [HD + 1, DK])
        v9 = sb("v9", [HD + 1, 2 * DK])
        qT = sb("qT", [DK, HD + 1])
        kT = sb("kT", [DK, HD + 1])
        vT = sb("vT", [P, HD + 1])
        qT_rep = sb("qT_rep", [DK, H, HD])
        bq_rep = sb("bq_rep", [DK, P])
        bv_rep = sb("bv_rep", [P, P])
        wv_diag = sb("wv_diag", [P, HD * (P + H)])
        wo_sb = sb("wo_sb", [P, HD, P])
        bo_b = sb("bo_b", [P, P])
        out_bias = sb("out_bias", [P, P])
        q_proj = sb("q_proj", [P, HD + 1, H])
        q_bias = sb("q_bias", [P, HD + 1, H])
        o_proj = sb("o_proj", [P, P])
        router = sb("router", [P, E])

        x_sb = sb("x_sb", [P, NT, P])
        ctx_sb = sb("ctx_sb", [P, NT, P])
        ctx_ig = sb("ctx_ig", [P, NT, HD, H])
        xb = sb("xb", [P, NT, P])
        x2 = sb("x2", [P, NT, P])
        stats = sb("stats", [P, NT, 6])
        mv = sb("mv", [P, NT, 2])
        rstd = sb("rstd", [P, NT])
        shift = sb("shift", [P, NT])
        vtmp = sb("vtmp", [P, NT])

        xn = sb("xn", [P, 2, P])
        xnT = sb("xnT", [P, 2, P])
        q_sb = sb("q_sb", [P, 2, HD + 1, H])
        qk = sb("qk", [P, 2, HD, H * H])
        neg_max = sb("neg_max", [P, 2, H])
        shifted = sb("shifted", [P, 2, H, H])
        probs = sb("probs", [P, 2, H, H])
        rowsum = sb("rowsum", [P, 2, H])
        rowinv = sb("rowinv", [P, 2, H])
        pv = sb("pv", [P, 2, H * HD, H])
        z0 = sb("z0", [P, 2, P])
        z = sb("z", [P, 2, P])
        zT = sb("zT", [P, 2, P])

        stats2 = sb("stats2", [P, G, 6])
        mv2 = sb("mv2", [P, G, 2])
        vtmp2 = sb("vtmp2", [P, G])
        rstd2 = sb("rstd2", [P, G])
        shift2 = sb("shift2", [P, G])
        rows = sb("rows", [P, G, TOP, ROWW])
        dest = sb("dest", [P, NT, TOP])
        gates = sb("gates", [P, TOP, G])
        rows_i = rows[:, :, :, :].bitcast(I32)
        xn2 = sb("xn2", [P, G, P])
        xn2T = sb("xn2T", [P, G, P])
        r1 = sb("r1", [P, G])
        r2 = sb("r2", [P, G, E])
        r3 = sb("r3", [P, G, E])
        route_p = sb("route_p", [P, G, E])
        eq = sb("eq", [P, G, E])
        best = sb("best", [P, G])
        pick = sb("pick", [P, TOP, G, E])
        picked = sb("picked", [P, G, E])
        group_sum = sb("group_sum", [P, E])
        carry = sb("carry", [P, E])
        slot = sb("slot", [P, G, E])
        slot_of = sb("slot_of", [P, G, E])
        place = sb("place", [P, G, TOP])
        pos = sb("pos", [P, G, TOP], I32)

        over = sb("over", [P, E, NT])
        n_tiles = sb("n_tiles", [P, E])
        tile_end = sb("tile_end", [P, E])
        jump = sb("jump", [P, E])
        passed = sb("passed", [P, TILES, E])
        jumps = sb("jumps", [P, TILES, E])
        tile_e = sb("tile_e", [P, TILES])
        tile_row = sb("tile_row", [P, TILES])
        w_off = sb("w_off", [P, TILES], I32)
        s_off = sb("s_off", [P, TILES], I32)
        row_off = sb("row_off", [P, TILES], I32)
        pad_off = sb("pad_off", [P, E], I32)

        w_sb = sb("w_sb", [P, 2 * E, F])
        w_scale = sb("w_scale", [P, 2 * E, F])
        w1_sb = sb("w1_sb", [P, E * F])
        s1_sb = wo_sb[:, :, :].rearrange("p c n -> p (c n)")
        xs = wv_diag[:, 0:XB * ROWW].rearrange("p (b n) -> p b n", b=XB)
        xsT = wv_diag[:, XB * ROWW:XB * ROWW + 2 * P].rearrange("p (b n) -> p b n", b=2)
        ctx_flat = ctx_sb[:, :, :].rearrange("p t n -> p (t n)")
        act_sb = ctx_flat[:, 0:2 * F].rearrange("p (b n) -> p b n", b=2)
        hid = ctx_flat[:, 2 * F:4 * F].rearrange("p (b n) -> p b n", b=2)
        x_flat = x_sb[:, :, :].rearrange("p t n -> p (t n)")
        hidT = x_flat[:, 0:2 * F].rearrange("p (b n) -> p b n", b=2)
        yo = x_flat[:, 2 * F:2 * F + XB * P].rearrange("p (b n) -> p b n", b=XB)
        xs_i = xs[:, :, :].bitcast(I32)
        got = pv[:, :, :, :].rearrange("p a (q m) g -> p (a q) (m g)", q=2)
        fin = qk[:, :, :, :].rearrange("p a (q i) s -> p (a q) (i s)", q=2)

        ld_small, ld_x, ld_ctx, ld_wo, ld_bo, ld_router = (sem(n) for n in (
            "ld_small", "ld_x", "ld_ctx", "ld_wo", "ld_bo", "ld_router"))
        ld_wv, ld_wg, ld_w1, ld_s1 = (sem(n) for n in ("ld_wv", "ld_wg", "ld_w1", "ld_s1"))
        pool_set = sem("pool_set")
        setup_pe, setup_dve, setup_step = sem("setup_pe"), sem("setup_dve"), sem("setup_step")
        ln1_mv, ln1_rstd, ln1_shift = sem("ln1_mv"), sem("ln1_rstd"), sem("ln1_shift")
        ln1_eps = sem("ln1_eps")
        ln1_stats = sem("ln1_stats")
        bias_ready, xb_ready, ctx_turned = sem("bias_ready"), sem("xb_ready"), sem("ctx_turned")
        xn_ready, xnT_psum, xnT_ready = sem("xn_ready"), sem("xnT_psum"), sem("xnT_ready")
        q_psum, q_ready, qk_ready = sem("q_psum"), sem("q_ready"), sem("qk_ready")
        s_psum, max_ready, s_shifted = sem("s_psum"), sem("max_ready"), sem("s_shifted")
        p_ready, sum_ready, inv_ready = sem("p_ready"), sem("sum_ready"), sem("inv_ready")
        pv_ready, z0_ready, z_ready = sem("pv_ready"), sem("z0_ready"), sem("z_ready")
        zT_psum, zT_ready, o_psum, x2_ready = (sem(n) for n in ("zT_psum", "zT_ready", "o_psum", "x2_ready"))
        st2_ready, w_scaled = sem("st2_ready"), sem("w_scaled")
        mv2_ready, eps2_ready, rstd2_ready, shift2_ready = (
            sem(n) for n in ("mv2_ready", "eps2_ready", "rstd2_ready", "shift2_ready"))
        xn2_ready, carry_ready, meta_ready = sem("xn2_ready"), sem("carry_ready"), sem("meta_ready")
        rows_ready, xn2T_psum, xn2T_ready, logits_psum = (
            sem(n) for n in ("rows_ready", "xn2T_psum", "xn2T_ready", "logits_psum"))
        logits_shifted, logits_exp, picked_ready, rank_psum, pos_ready = (
            sem(n) for n in ("logits_shifted", "logits_exp", "picked_ready", "rank_psum", "pos_ready"))
        route_step = sem("route_step")
        scattered = sem("scattered")
        counts_psum, table_step, table_ready, padded = (
            sem(n) for n in ("counts_psum", "table_step", "table_ready", "padded"))
        xs_loaded = [sem(f"xs_loaded{b}") for b in range(XB)]
        y_sent = [sem(f"y_sent{b}") for b in range(XB)]
        xsT_psum, xsT_ready, gate_psum, val_psum = (
            sem(n) for n in ("xsT_psum", "xsT_ready", "gate_psum", "val_psum"))
        act_ready, hid_ready, hidT_psum, hidT_ready = (
            sem(n) for n in ("act_ready", "hid_ready", "hidT_psum", "hidT_ready"))
        y_psum, yo_ready = sem("y_psum"), sem("yo_ready")
        got_rows = [sem(f"got_rows{g}") for g in range(NG)]
        pair_sum, fin_ready, stored = sem("pair_sum"), sem("fin_ready"), sem("stored")

        POOL_SET = 16
        AHEAD = 2

        def tile_at(g, j, lag):
            t = g * G + (AHEAD + j - lag)
            if isinstance(t, int) and not 0 <= t < NT:
                return None
            return t, (AHEAD + j - lag) % 2

        def group_at(g, j, lag):
            if (AHEAD + j - lag) % G:
                return None
            n = g + (AHEAD + j - lag) // G
            return None if isinstance(n, int) and not 0 <= n < NG else (n,)

        def second_on(t):
            return not isinstance(t, int) or t >= 2

        def first_on(t):
            return not isinstance(t, int) or t >= 1

        def attention_steps(eng, step):
            for g in (-1, 0):
                for j in range(G):
                    step(g, j)
            with eng.Fori(1, NG - 1) as g:
                for j in range(G):
                    step(g, j)
            for g in (NG - 1, NG):
                for j in range(G):
                    step(g, j)

        SENT = 16 * G * TOP
        full = (TILES - 3) // XB
        assert TILES - 3 == full * XB

        def ffn_steps(eng, step):
            for k in range(-3, XB):
                step(0, k)
            with eng.Fori(1, full) as i:
                for k in range(XB):
                    step(i, k)
            for k in range(3):
                step(full, k)

        def ffn_tile(i, k, ahead):
            c = 1 + k + ahead
            if isinstance(i, int) and not 0 <= i * XB + c < TILES:
                return None
            return i * XB + c, c, i

        def uses(i, c):
            return i + (c // XB + 1)

        with nc.Block() as block:

            @block.sync
            def _(sp):
                for k in range(0, NT, G):
                    sp.dma_start(x_sb[:, k:k + G, :], x.rearrange("t p d -> p t d")[:, k:k + G, :]).then_inc(ld_x, 16)
                sp.dma_start(wo_sb[:, :, :], Wo.rearrange("(c p) n -> p c n", p=P)).then_inc(ld_wo, 16)
                sp.dma_start(bo_b[:, :], bo.partition_broadcast(P)).then_inc(ld_bo, 16)
                sp.dma_start(router[:, :], router_w).then_inc(ld_router, 16)
                for half, (weight, scale, ld) in enumerate(((wv, sv, ld_wv), (w, s, ld_wg))):
                    at = slice(half * E, half * E + E)
                    sp.dma_start(w_sb[:, at, :], weight.rearrange("e d f -> d e f")).then_inc(ld, 16)
                    sp.dma_start(w_scale[:, at, :].rearrange("p e f -> p (e f)"),
                                 scale.rearrange("e a f -> (e a f)").partition_broadcast(P)).then_inc(ld, 16)
                sp.dma_start(w1_sb[:, :].rearrange("p (e c n) -> p e c n", e=E, c=FC),
                             w1.rearrange("e (c p) n -> p e c n", p=P)).then_inc(ld_w1, 16)
                sp.wait_ge(setup_pe, 3)
                sp.dma_start(s1_sb[:, :], s1.rearrange("e a n -> (e a n)").partition_broadcast(P)).then_inc(ld_s1, 16)

                sp.wait_ge(table_ready, 1)
                for e in range(E):
                    r0 = sp.value_load(pad_off[0:1, e:e + 1], min_val=0, max_val=ROWS - P)
                    sp.dma_start(routed[bass.ds(r0, P), :], pad_rows[:, :]).then_inc(padded, 16)
                sp.wait_ge(padded, 16 * E)
                sp.wait_ge(scattered, SENT * (NG + 1))

                def load(i, c):
                    if not (isinstance(i, int) and i == 0):
                        sp.wait_ge(y_sent[c], 16 * i)
                    r0 = sp.value_load(row_off[0:1, bass.ds(i * XB + c, 1)], min_val=0, max_val=ROWS - P)
                    sp.dma_start(xs[:, c, :], routed[bass.ds(r0, P), :]).then_inc(xs_loaded[c], 16)

                whole = TILES // XB
                for c in range(XB):
                    load(0, c)
                with sp.Fori(1, whole) as i:
                    for c in range(XB):
                        load(i, c)
                for c in range(TILES - whole * XB):
                    load(whole, c)

                for b in range(XB):
                    sp.wait_ge(y_sent[b], 16 * len(range(b, TILES, XB)))
                pairs = expert_out.rearrange("(t p k) d -> p t (k d)", p=P, k=TOP)
                for g in range(NG):
                    sp.dma_start(got[:, g, :].rearrange("p (t n) -> p t n", t=G),
                                 pairs[:, G * g:G * g + G, :]).then_inc(got_rows[g], 16)
                for g in range(NG):
                    sp.wait_ge(fin_ready, g + 1)
                    sp.dma_start(out.rearrange("t p d -> p t d")[:, G * g:G * g + G, :],
                                 x2[:, G * g:G * g + G, :]).then_inc(stored, 16)
                sp.wait_ge(stored, 16 * NG)

            @block.gpsimd
            def _(pool):
                last_row, last_dest = pool.to_reg(ROWS - 1), pool.to_reg(TOP * TOKENS - 1)
                steps = [0]

                def built(ins):
                    steps[0] += 1
                    ins.then_inc(pool_set, 1)
                    pool.wait_ge(pool_set, steps[0])

                built(pool.memset(ident[:, :], 0.0))
                built(pool.affine_select(out=ident[:, :], in_=ident[:, :], compare_op=ALU.not_equal, fill=1.0,
                                         base=0, pattern=[[-1, P]], channel_multiplier=1))
                built(pool.memset(head_mask[:, :], SCALE))
                built(pool.affine_select(out=head_mask[:, :], in_=head_mask[:, :], compare_op=ALU.is_ge, fill=0.0,
                                         base=0, pattern=[[-HD, H]], channel_multiplier=1))
                built(pool.affine_select(out=head_mask[:, :], in_=head_mask[:, :], compare_op=ALU.is_ge, fill=0.0,
                                         base=HD - 1, pattern=[[HD, H]], channel_multiplier=-1))
                built(pool.memset(minus_half[:, :], -0.5))
                built(pool.memset(eps[:, :], EPS))
                built(pool.memset(ones[:, :], 1.0))
                built(pool.affine_select(out=before[:, :], in_=ones[:, :], compare_op=ALU.is_ge, fill=0.0,
                                         base=-1, pattern=[[1, P]], channel_multiplier=-1))
                built(pool.iota(rev[:, :, :], pattern=[[0, G], [-1, E]], base=E, channel_multiplier=0,
                                allow_small_or_imprecise_dtypes=True))
                built(pool.iota(region0[:, :, :], pattern=[[0, G], [REGION, E]], base=0, channel_multiplier=0,
                                allow_small_or_imprecise_dtypes=True))
                built(pool.iota(dest[:, :, :], pattern=[[TOP * P, NT], [1, TOP]], base=0, channel_multiplier=TOP,
                                allow_small_or_imprecise_dtypes=True))
                built(pool.iota(tile_edges[:, :, :], pattern=[[0, E], [P, NT]], base=0, channel_multiplier=0,
                                allow_small_or_imprecise_dtypes=True))
                built(pool.iota(tile_no[:, :, :], pattern=[[1, TILES], [0, E]], base=0, channel_multiplier=0,
                                allow_small_or_imprecise_dtypes=True))
                built(pool.memset(pad_rows[:, :], 0.0))
                built(pool.iota(pad_rows[:, P:P + 1].bitcast(I32), pattern=[[0, 1]], base=NOWHERE, channel_multiplier=0))
                assert steps[0] == POOL_SET
                assert 16 * SPARE == SENT
                for n in range(SPARE):
                    r0 = E * REGION + n * P
                    pool.dma_start(routed[r0:r0 + P, :], pad_rows[:, :]).then_inc(scattered, 16)

                def carry_wait():
                    pool.tensor_tensor(pause_pool[:, :], eps[:, 0:1], eps[:, 0:1], ALU.add)

                pool.wait_ge(ln1_mv, NT)
                pool.tensor_tensor(vtmp[:, :], mv[:, :, 1], eps[:, :], ALU.add).then_inc(ln1_eps, 1)
                pool.wait_ge(ln1_eps, 1)
                pool.tensor_tensor(rstd[:, :], vtmp[:, :], minus_half[:, :], ALU.pow).then_inc(ln1_rstd, 1)
                pool.wait_ge(bias_ready, 1)
                pool.tensor_tensor(xb[:, :, :], x_sb[:, :, :],
                                   out_bias[:, :].unsqueeze(1).to_broadcast([P, NT, P]), ALU.add).then_inc(xb_ready, 1)

                def step(g, j):
                    if a := group_at(g, j, 7):
                        n, = a
                        pool.wait_ge(mv2_ready, n * G + G)
                        pool.tensor_tensor(vtmp2[:, :], mv2[:, :, 1], eps[:, 0:G], ALU.add).then_inc(eps2_ready, 1)
                        pool.wait_ge(eps2_ready, n + 1)
                        pool.tensor_tensor(rstd2[:, :], vtmp2[:, :], minus_half[:, 0:G], ALU.pow).then_inc(rstd2_ready, 1)
                    if a := tile_at(g, j, 1):
                        t, b = a
                        if isinstance(t, int) and t == 0:
                            pool.wait_ge(ctx_turned, NG)
                        pool.wait_ge(p_ready, t + 1)
                        if second_on(t):
                            pool.wait_ge(z0_ready, t - 1)
                        pool.tensor_tensor(
                            pv[:, b, :, :].rearrange("p (h i) g -> p h i g", h=H),
                            probs[:, b, :, :].unsqueeze(2).to_broadcast([P, H, HD, H]),
                            ctx_ig[:, t, :, :].unsqueeze(1).to_broadcast([P, H, HD, H]), ALU.mult).then_inc(pv_ready, 1)
                    if a := tile_at(g, j, 0):
                        t, _ = a
                        if isinstance(t, int) and t == 0:
                            pool.wait_ge(ld_wv, 32)
                        if (isinstance(t, int) and t == E) or (not isinstance(t, int) and (AHEAD + j) % G == 0):
                            pool.wait_ge(ld_wg, 32)
                        pool.tensor_tensor(w_sb[:, t, :], w_sb[:, t, :], w_scale[:, t, :], ALU.mult).then_inc(w_scaled, 1)
                    if a := group_at(g, j, 9):
                        n, = a
                        pool.wait_ge(rows_ready, (n + 2) * TOP)
                        pool.wait_ge(meta_ready, (n + 1) * 2)
                        pool.wait_ge(pos_ready, n + 2)
                        carry_wait()
                        for m in range(G):
                            for k in range(TOP):
                                pool.indirect_dma_start(
                                    out=routed[:, :],
                                    out_offset=bass.IndirectOffsetOnAxis(ap=pos[:, m, k:k + 1], axis=0),
                                    in_=rows[:, m, k, :], in_offset=None,
                                    bounds_check=last_row).then_inc(scattered, 16)

                attention_steps(pool, step)

                for t in range(TILES):
                    pool.wait_ge(yo_ready, t + 1)
                    pool.indirect_dma_start(
                        out=expert_out[:, :],
                        out_offset=bass.IndirectOffsetOnAxis(ap=xs_i[:, t % XB, P:P + 1], axis=0),
                        in_=yo[:, t % XB, :], in_offset=None,
                        bounds_check=last_dest, oob_is_err=False).then_inc(y_sent[t % XB], 16)

            @block.scalar
            def _(act):
                act.sem_inc(xn2T_ready, 1)
                act.sem_inc(rows_ready, TOP)
                for to, frm in ((q9[0:HD, :], Wq), (q9[HD:HD + 1, :], bq.unsqueeze(0)),
                                (k9[0:HD, :], Wk), (k9[HD:HD + 1, :], bk.unsqueeze(0)),
                                (v9[0:HD, 0:DK], Wv), (v9[0:HD, DK:2 * DK], Wv),
                                (v9[HD:HD + 1, 0:DK], bv.unsqueeze(0)), (v9[HD:HD + 1, DK:2 * DK], bv.unsqueeze(0))):
                    act.dma_start(to, frm).then_inc(ld_small, 16)
                for k in range(0, NT, G):
                    act.dma_start(ctx_sb[:, k:k + G, :], ctx.rearrange("t p d -> p t d")[:, k:k + G, :]).then_inc(ld_ctx, 16)

                act.wait_ge(ld_ctx, 16 * NG)
                for k in range(0, NT, G):
                    nc.scalar.copy(ctx_ig[:, k:k + G, :, :],
                                   ctx_sb[:, k:k + G, :].rearrange("p t (h i) -> p t i h", h=H)).then_inc(ctx_turned, 1)

                def step(g, j):
                    if a := tile_at(g, j, -2):
                        t, b = a
                        if isinstance(t, int) and t == 0:
                            act.wait_ge(ln1_shift, 1)
                        if second_on(t):
                            act.wait_ge(xnT_psum, t - 1)
                        nc.scalar.activation(xn[:, b, :], x_sb[:, t, :], ACT.Identity, scale=rstd[:, bass.ds(t, 1)],
                                             bias=shift[:, bass.ds(t, 1)]).then_inc(xn_ready, 1)
                    if a := tile_at(g, j, 1):
                        t, b = a
                        act.wait_ge(s_shifted, t + 1)
                        if second_on(t):
                            act.wait_ge(pv_ready, t - 1)
                            act.wait_ge(sum_ready, t - 1)
                        nc.scalar.activation(probs[:, b, :, :], shifted[:, b, :, :], ACT.Exp).then_inc(p_ready, 1)
                    if a := tile_at(g, j, -1):
                        t, b = a
                        act.wait_ge(xnT_psum, t + 1)
                        if second_on(t):
                            act.wait_ge(q_psum, t - 1)
                        nc.scalar.copy(xnT[:, b, :], bank[0][:, 0:P]).then_inc(xnT_ready, 1)
                    if a := tile_at(g, j, 2):
                        t, b = a
                        act.wait_ge(zT_psum, t + 1)
                        if second_on(t):
                            act.wait_ge(o_psum, t - 1)
                        nc.scalar.copy(zT[:, b, :], bank[4][:, 0:P]).then_inc(zT_ready, 1)
                    if a := tile_at(g, j, 2):
                        t, b = a
                        act.wait_ge(o_psum, t + 1)
                        nc.scalar.copy(x2[:, t, :], bank[5][:, 0:P]).then_inc(x2_ready, 1)
                    if a := group_at(g, j, 7):
                        n, = a
                        act.wait_ge(shift2_ready, n + 1)
                        act.wait_ge(rows_ready, (n + 1) * TOP)
                        act.wait_ge(xn2T_psum, n + 1)
                        for m in range(G):
                            t = n * G + m
                            nc.scalar.activation(xn2[:, m, :], x2[:, t, :], ACT.Identity, scale=rstd2[:, m:m + 1],
                                                 bias=shift2[:, m:m + 1]).then_inc(xn2_ready, 1)
                    if a := group_at(g, j, 7):
                        n, = a
                        act.wait_ge(xn2T_psum, n + 2)
                        act.wait_ge(logits_psum, n + 1)
                        nc.scalar.copy(xn2T[:, :, :].rearrange("p t n -> p (t n)"), bank[6][:, :]).then_inc(xn2T_ready, 1)
                    if a := group_at(g, j, 8):
                        n, = a
                        act.wait_ge(logits_shifted, n + 1)
                        nc.scalar.activation(r3[:, :, :], r2[:, :, :], ACT.Exp).then_inc(logits_exp, 1)
                    if a := group_at(g, j, 9):
                        n, = a
                        act.wait_ge(xn2_ready, n * G + G)
                        act.wait_ge(scattered, (n + 1) * SENT)
                        for k in range(TOP):
                            nc.scalar.copy(rows[:, :, k, 0:P], xn2[:, :, :]).then_inc(rows_ready, 1)

                attention_steps(act, step)

                def ffn(i, k):
                    if a := ffn_tile(i, k, 2):
                        t, c, _ = a
                        act.wait_ge(xsT_psum, t + 1)
                        if second_on(t):
                            act.wait_ge(val_psum, t - 1)
                        nc.scalar.copy(xsT[:, c % 2, :], bank[0][:, 0:P]).then_inc(xsT_ready, 1)
                    if a := ffn_tile(i, k, 1):
                        t, c, _ = a
                        act.wait_ge(gate_psum, t + 1)
                        if second_on(t):
                            act.wait_ge(hid_ready, t - 1)
                        nc.scalar.activation(act_sb[:, c % 2, :], bank[1 + c % 2][:, :],
                                             ACT.Gelu_apprx_tanh).then_inc(act_ready, 1)
                    if a := ffn_tile(i, k, 0):
                        t, c, _ = a
                        act.wait_ge(hidT_psum, t + 1)
                        if second_on(t):
                            act.wait_ge(y_psum, t - 1)
                        nc.scalar.copy(hidT[:, c % 2, :], bank[5][:, :]).then_inc(hidT_ready, 1)

                ffn_steps(act, ffn)

            @block.tensor
            def _(pe):
                pe.sem_inc(logits_psum, 1)
                pe.sem_inc(xn2T_psum, 1)
                pe.wait_ge(pool_set, 2)
                pe.wait_ge(ld_small, 16 * 8)
                nc.tensor.transpose(bank[0][0:DK, 0:HD + 1], q9[:, :], ident[0:HD + 1, 0:HD + 1])
                nc.tensor.transpose(bank[0][0:DK, 16:17 + HD], k9[:, :], ident[0:HD + 1, 0:HD + 1])
                nc.tensor.transpose(bank[0][:, 32:33 + HD], v9[:, :], ident[0:HD + 1, 0:HD + 1]).then_inc(setup_pe, 1)
                pe.wait_ge(setup_dve, 1)
                nc.tensor.matmul(bank[1][:, 0:HD + 1], qT_rep[:, :, :].rearrange("p h i -> p (h i)"), kT[:, :],
                                 start=True, stop=True)
                nc.tensor.matmul(bank[1][:, 16:17 + HD], bq_rep[:, :], kT[:, :], start=True, stop=True).then_inc(setup_pe, 1)
                pe.wait_ge(setup_dve, 2)
                pe.wait_ge(ld_wo, 16)
                for c in range(HD):
                    nc.tensor.matmul(bank[4][:, 0:P], wv_diag[:, c * P:c * P + P], wo_sb[:, c, :],
                                     start=(c == 0), stop=(c == HD - 1))
                for c in range(HD):
                    mm = nc.tensor.matmul(bank[5][:, 0:P], bv_rep[:, :], wo_sb[:, c, :],
                                          start=(c == 0), stop=(c == HD - 1))
                mm.then_inc(setup_pe, 1)
                pe.wait_ge(setup_dve, 5)

                def step(g, j):
                    if a := tile_at(g, j, 0):
                        t, b = a
                        pe.wait_ge(qk_ready, t + 1)
                        if second_on(t):
                            pe.wait_ge(s_shifted, t - 1)
                        nc.tensor.matmul(bank[2 + b][:, 0:H * H], ident[:, :],
                                         q_sb[:, b, HD, :].unsqueeze(2).to_broadcast([P, H, H]), start=True, stop=False)
                        for i in range(HD):
                            mm = nc.tensor.matmul(bank[2 + b][:, 0:H * H], ident[:, :], qk[:, b, i, :],
                                                  start=False, stop=(i == HD - 1))
                        mm.then_inc(s_psum, 1)
                    if a := group_at(g, j, 8):
                        n, = a
                        pe.wait_ge(xn2T_ready, n + 2)
                        if isinstance(n, int) and n == 0:
                            pe.wait_ge(ld_router, 16)
                        pe.wait_ge(pos_ready, n + 1)
                        for m in range(G):
                            mm = nc.tensor.matmul(bank[7][:, m * E:m * E + E], xn2T[:, m, :], router[:, :],
                                                  start=True, stop=True)
                        mm.then_inc(logits_psum, 1)
                    if a := group_at(g, j, 9):
                        n, = a
                        pe.wait_ge(picked_ready, n + 1)
                        rank = bank[7][:, 64:64 + G * E]
                        flat = picked[:, :, :].rearrange("p t e -> p (t e)")
                        nc.tensor.matmul(rank, before[:, :], flat, start=True, stop=False)
                        for m in range(1, G):
                            nc.tensor.matmul(rank[:, m * E:], ones[:, :], flat[:, 0:(G - m) * E], start=False, stop=False)
                        nc.tensor.matmul(rank, ones[:, :], carry[:, :].unsqueeze(1).to_broadcast([P, G, E]),
                                         start=False, stop=True).then_inc(rank_psum, 1)
                    if a := tile_at(g, j, -2):
                        t, b = a
                        pe.wait_ge(xn_ready, t + 1)
                        if first_on(t):
                            pe.wait_ge(xnT_ready, t)
                        nc.tensor.transpose(bank[0][:, 0:P], xn[:, b, :], ident[:, :]).then_inc(xnT_psum, 1)
                    if a := tile_at(g, j, 2):
                        t, b = a
                        pe.wait_ge(z_ready, t + 1)
                        if first_on(t):
                            pe.wait_ge(zT_ready, t)
                        nc.tensor.transpose(bank[4][:, 0:P], z[:, b, :], ident[:, :]).then_inc(zT_psum, 1)
                    if a := tile_at(g, j, -1):
                        t, b = a
                        pe.wait_ge(xnT_ready, t + 1)
                        if first_on(t):
                            pe.wait_ge(q_ready, t)
                        nc.tensor.matmul(bank[1][:, 0:QW], xnT[:, b, :], q_proj[:, :, :].rearrange("p i h -> p (i h)"),
                                         start=True, stop=True).then_inc(q_psum, 1)
                    if a := tile_at(g, j, 2):
                        t, b = a
                        pe.wait_ge(zT_ready, t + 1)
                        if isinstance(t, int) and t == 0:
                            pe.wait_ge(xb_ready, 1)
                        if first_on(t):
                            pe.wait_ge(x2_ready, t)
                        nc.tensor.matmul(bank[5][:, 0:P], zT[:, b, :], o_proj[:, :], start=True, stop=False)
                        nc.tensor.matmul(bank[5][:, 0:P], ident[:, :], xb[:, t, :], start=False, stop=True).then_inc(o_psum, 1)
                    if a := group_at(g, j, 7):
                        n, = a
                        pe.wait_ge(xn2T_ready, n + 1)
                        for m in range(G):
                            pe.wait_ge(xn2_ready, n * G + (m + 1))
                            mm = nc.tensor.transpose(bank[6][:, m * P:m * P + P], xn2[:, m, :], ident[:, :])
                        mm.then_inc(xn2T_psum, 1)

                attention_steps(pe, step)

                pe.wait_ge(carry_ready, NG)
                nc.tensor.matmul(bank[6][:, 0:E], ones[:, :], carry[:, :], start=True, stop=True).then_inc(counts_psum, 1)
                pe.wait_ge(table_ready, 1)
                pe.wait_ge(w_scaled, 2 * E)
                pe.wait_ge(ld_w1, 16)
                w_flat = w_sb[:, :, :].rearrange("p e f -> p (e f)")

                def ffn(i, k):
                    if a := ffn_tile(i, k, 2):
                        t, c, r = a
                        pe.wait_ge(xs_loaded[c % XB], uses(r, c) * 16)
                        if first_on(t):
                            pe.wait_ge(xsT_ready, t)
                        nc.tensor.transpose(bank[0][:, 0:P], xs[:, c % XB, 0:P], ident[:, :]).then_inc(xsT_psum, 1)
                    if a := ffn_tile(i, k, 1):
                        t, c, _ = a
                        off = pe.value_load(w_off[0:1, bass.ds(t, 1)], min_val=0, max_val=(E - 1) * F)
                        pe.wait_ge(xsT_ready, t + 1)
                        if second_on(t):
                            pe.wait_ge(hid_ready, t - 1)
                        nc.tensor.matmul(bank[1 + c % 2][:, :], xsT[:, c % 2, :], w_flat[:, bass.ds(off + E * F, F)],
                                         start=True, stop=True).then_inc(gate_psum, 1)
                        nc.tensor.matmul(bank[3 + c % 2][:, :], xsT[:, c % 2, :], w_flat[:, bass.ds(off, F)],
                                         start=True, stop=True).then_inc(val_psum, 1)
                    if a := ffn_tile(i, k, -1):
                        t, c, _ = a
                        off = pe.value_load(w_off[0:1, bass.ds(t, 1)], min_val=0, max_val=(E - 1) * F)
                        pe.wait_ge(hidT_ready, t + 1)
                        if first_on(t):
                            pe.wait_ge(yo_ready, t)
                        for n in range(FC):
                            mm = nc.tensor.matmul(bank[6][:, 0:P], hidT[:, c % 2, n * P:n * P + P],
                                                  w1_sb[:, bass.ds(off + n * P, P)], start=(n == 0), stop=(n == FC - 1))
                        mm.then_inc(y_psum, 1)
                    if a := ffn_tile(i, k, 0):
                        t, c, _ = a
                        pe.wait_ge(hid_ready, t + 1)
                        if first_on(t):
                            pe.wait_ge(hidT_ready, t)
                        for n in range(FC):
                            mm = nc.tensor.transpose(bank[5][:, n * P:n * P + P], hid[:, c % 2, n * P:n * P + P], ident[:, :])
                        mm.then_inc(hidT_psum, 1)

                ffn_steps(pe, ffn)

            @block.vector
            def _(dve):
                v = nc.vector
                chain = [0]

                def small(ins):
                    chain[0] += 1
                    ins.then_inc(setup_step, 1)
                    dve.wait_ge(setup_step, chain[0])

                dve.sem_inc(pos_ready, 1)
                small(v.memset(wv_diag[:, :], 0.0))
                small(v.memset(carry[:, :], 0.0))
                dve.wait_ge(setup_pe, 1)
                small(v.tensor_copy(qT_rep[:, :, :], bank[0][0:DK, 0:HD].unsqueeze(1).to_broadcast([DK, H, HD])))
                small(v.tensor_copy(bq_rep[:, :], bank[0][0:DK, HD:HD + 1].to_broadcast([DK, P])))
                v.tensor_copy(kT[:, :], bank[0][0:DK, 16:17 + HD]).then_inc(setup_dve, 1)
                small(v.tensor_copy(bv_rep[:, :], bank[0][:, 32 + HD:33 + HD].to_broadcast([P, P])))
                for a in range(2):
                    at = slice(a * DK, a * DK + DK)
                    ins = v.tensor_copy(wv_diag[at, :].rearrange("p (c k) -> p c k", c=HD)[:, :, a * HD:a * HD + HD],
                                        bank[0][at, 32:32 + HD].unsqueeze(1).to_broadcast([DK, HD, HD]))
                    if a == 0:
                        small(ins)
                ins.then_inc(setup_dve, 1)
                dve.wait_ge(ld_x, 16 * NG)
                for t in range(NT):
                    v.bn_stats(stats[:, t, :], x_sb[:, t, :]).then_inc(ln1_stats, 1)
                for t in range(NT):
                    dve.wait_ge(ln1_stats, t + 1)
                    v.bn_aggr(mv[:, t, :], stats[:, t, :]).then_inc(ln1_mv, 1)
                dve.wait_ge(setup_pe, 2)
                dve.wait_ge(pool_set, POOL_SET)
                v.tensor_tensor(q_proj[:, :, :], bank[1][:, 0:HD + 1].unsqueeze(2).to_broadcast([P, HD + 1, H]),
                                head_mask[:, :].unsqueeze(1).to_broadcast([P, HD + 1, H]), ALU.mult).then_inc(setup_dve, 1)
                v.tensor_scalar(q_bias[:, :, :], bank[1][:, 16:17 + HD].unsqueeze(2).to_broadcast([P, HD + 1, H]),
                                SCALE, None, ALU.mult).then_inc(setup_dve, 1)
                dve.wait_ge(ln1_rstd, 1)
                dve.wait_ge(ln1_mv, NT)
                v.scalar_tensor_tensor(shift[:, :], mv[:, :, 0], -1.0, rstd[:, :], ALU.mult, ALU.mult).then_inc(ln1_shift, 1)
                dve.wait_ge(setup_pe, 3)
                dve.wait_ge(ld_bo, 16)
                v.tensor_tensor(out_bias[:, :], bank[5][:, 0:P], bo_b[:, :], ALU.add).then_inc(bias_ready, 1)
                v.tensor_copy(o_proj[:, :], bank[4][:, 0:P]).then_inc(setup_dve, 1)
                dve.wait_ge(ctx_turned, NG)
                dve.wait_ge(setup_dve, 5)

                CHAIN = 21

                def step(g, j):
                    done = [0]

                    def routed_step(n, ins):
                        done[0] += 1
                        ins.then_inc(route_step, 1)
                        dve.wait_ge(route_step, n * CHAIN + done[0])

                    def wide(x):
                        return x.unsqueeze(2).to_broadcast([P, G, E])

                    if a := tile_at(g, j, 0):
                        t, b = a
                        dve.wait_ge(q_psum, t + 1)
                        if second_on(t):
                            dve.wait_ge(s_psum, t - 1)
                        v.tensor_tensor(q_sb[:, b, :, :], bank[1][:, 0:QW].rearrange("p (i h) -> p i h", h=H),
                                        q_bias[:, :, :], ALU.add).then_inc(q_ready, 1)
                        dve.wait_ge(q_ready, t + 1)
                        v.tensor_tensor(qk[:, b, :, :].rearrange("p i (h g) -> p i h g", h=H),
                                        q_sb[:, b, 0:HD, :].unsqueeze(3).to_broadcast([P, HD, H, H]),
                                        ctx_ig[:, t, :, :].unsqueeze(2).to_broadcast([P, HD, H, H]),
                                        ALU.mult).then_inc(qk_ready, 1)
                    if a := tile_at(g, j, 1):
                        t, b = a
                        dve.wait_ge(s_psum, t + 1)
                        scores = bank[2 + b][:, 0:H * H].rearrange("p (h g) -> p h g", h=H)
                        v.tensor_reduce(neg_max[:, b, :], scores, AX_X, ALU.max, negate=True).then_inc(max_ready, 1)
                        dve.wait_ge(max_ready, t + 1)
                        if second_on(t):
                            dve.wait_ge(p_ready, t - 1)
                        v.tensor_tensor(shifted[:, b, :, :], scores,
                                        neg_max[:, b, :].unsqueeze(2).to_broadcast([P, H, H]), ALU.add).then_inc(s_shifted, 1)
                    if a := group_at(g, j, 9):
                        n, = a
                        done[0] = 1
                        dve.wait_ge(logits_exp, n + 1)
                        routed_step(n, v.tensor_reduce(r1[:, :], r3[:, :, :], AX_X, ALU.add))
                        routed_step(n, v.reciprocal(r1[:, :], r1[:, :]))
                        routed_step(n, v.tensor_tensor(route_p[:, :, :], r3[:, :, :], wide(r1[:, :]), ALU.mult))
                        for k in range(TOP):
                            gate = gates[:, k, :]
                            routed_step(n, v.tensor_reduce(gate, route_p[:, :, :], AX_X, ALU.max))
                            routed_step(n, v.tensor_tensor(eq[:, :, :], route_p[:, :, :], wide(gate), ALU.is_equal))
                            routed_step(n, v.tensor_tensor(eq[:, :, :], eq[:, :, :], rev[:, :, :], ALU.mult))
                            routed_step(n, v.tensor_reduce(best[:, :], eq[:, :, :], AX_X, ALU.max))
                            routed_step(n, v.tensor_tensor(pick[:, k, :, :], rev[:, :, :], wide(best[:, :]), ALU.is_equal))
                            if k == 0:
                                routed_step(n, v.scalar_tensor_tensor(route_p[:, :, :], pick[:, k, :, :], -2.0,
                                                                      route_p[:, :, :], ALU.mult, ALU.add))
                        v.tensor_tensor(picked[:, :, :], pick[:, 0, :, :], pick[:, 1, :, :], ALU.add).then_inc(picked_ready, 1)
                    if a := tile_at(g, j, 2):
                        t, b = a
                        dve.wait_ge(pv_ready, t + 1)
                        v.tensor_reduce(z0[:, b, :], pv[:, b, :, :], AX_X, ALU.add).then_inc(z0_ready, 1)
                    if a := tile_at(g, j, 1):
                        t, b = a
                        dve.wait_ge(p_ready, t + 1)
                        v.tensor_reduce(rowsum[:, b, :], probs[:, b, :, :], AX_X, ALU.add).then_inc(sum_ready, 1)
                        dve.wait_ge(sum_ready, t + 1)
                        v.reciprocal(rowinv[:, b, :], rowsum[:, b, :]).then_inc(inv_ready, 1)
                    if a := tile_at(g, j, 2):
                        t, b = a
                        dve.wait_ge(z0_ready, t + 1)
                        dve.wait_ge(inv_ready, t + 1)
                        if second_on(t):
                            dve.wait_ge(zT_psum, t - 1)
                        v.tensor_tensor(z[:, b, :].rearrange("p (h i) -> p h i", h=H),
                                        z0[:, b, :].rearrange("p (h i) -> p h i", h=H),
                                        rowinv[:, b, :].unsqueeze(2).to_broadcast([P, H, HD]), ALU.mult).then_inc(z_ready, 1)
                    if a := group_at(g, j, 7):
                        n, = a
                        dve.wait_ge(rstd2_ready, n + 1)
                        v.scalar_tensor_tensor(shift2[:, :], mv2[:, :, 0], -1.0, rstd2[:, :],
                                               ALU.mult, ALU.mult).then_inc(shift2_ready, 1)
                    if a := tile_at(g, j, 3):
                        t, b = a
                        dve.wait_ge(x2_ready, t + 1)
                        m = (AHEAD + j - 3) % G
                        v.bn_stats(stats2[:, m, :], x2[:, t, :]).then_inc(st2_ready, 1)
                        dve.wait_ge(st2_ready, t + 1)
                        v.memset(pause_dve[:, :], 0.0)
                        v.bn_aggr(mv2[:, m, :], stats2[:, m, :]).then_inc(mv2_ready, 1)
                    if a := group_at(g, j, 8):
                        n, = a
                        dve.wait_ge(logits_psum, n + 2)
                        logits = bank[7][:, 0:G * E].rearrange("p (t e) -> p t e", t=G)
                        routed_step(n, v.tensor_reduce(r1[:, :], logits, AX_X, ALU.max, negate=True))
                        v.tensor_tensor(r2[:, :, :], logits, wide(r1[:, :]), ALU.add).then_inc(logits_shifted, 1)
                    if a := group_at(g, j, 9):
                        n, = a
                        done[0] = 15
                        dve.wait_ge(rank_psum, n + 1)
                        dve.wait_ge(scattered, (n + 1) * SENT)
                        v.tensor_copy(rows_i[:, :, :, P], dest[:, bass.ds(n * G, G), :]).then_inc(meta_ready, 1)
                        v.tensor_copy(rows[:, :, :, P + 1].rearrange("p t k -> p k t"), gates[:, :, :]).then_inc(meta_ready, 1)
                        rank = bank[7][:, 64:64 + G * E].rearrange("p (t e) -> p t e", t=G)
                        routed_step(n, v.tensor_tensor(slot[:, :, :], rank, region0[:, :, :], ALU.add))
                        for k in range(TOP):
                            routed_step(n, v.tensor_tensor(slot_of[:, :, :], slot[:, :, :], pick[:, k, :, :], ALU.mult))
                            routed_step(n, v.tensor_reduce(place[:, :, k], slot_of[:, :, :], AX_X, ALU.add))
                        v.tensor_copy(pos[:, :, :], place[:, :, :]).then_inc(pos_ready, 1)
                        routed_step(n, v.tensor_reduce(group_sum[:, :], picked[:, :, :].rearrange("p t e -> p e t"), AX_X, ALU.add))
                        v.tensor_tensor(carry[:, :], carry[:, :], group_sum[:, :], ALU.add).then_inc(carry_ready, 1)
                        dve.wait_ge(carry_ready, n + 1)
                        assert done[0] == CHAIN, done

                attention_steps(dve, step)
                tab = [0]

                def table(ins):
                    tab[0] += 1
                    ins.then_inc(table_step, 1)
                    dve.wait_ge(table_step, tab[0])

                dve.wait_ge(counts_psum, 1)
                counts = bank[6][:, 0:E]
                table(v.tensor_tensor(pad_off[:, :], counts, region0[:, 0, :], ALU.add))
                table(v.tensor_tensor(over[:, :, :], counts.unsqueeze(2).to_broadcast([P, E, NT]), tile_edges[:, :, :], ALU.is_gt))
                table(v.tensor_reduce(n_tiles[:, :], over[:, :, :], AX_X, ALU.add))
                table(v.tensor_tensor_scan(tile_end[:, :], ones[:, 0:E], n_tiles[:, :], 0.0, ALU.mult, ALU.add))
                table(v.tensor_scalar(jump[:, :], n_tiles[:, :], -float(P), float(REGION), ALU.mult, ALU.add))
                table(v.tensor_tensor(passed[:, :, :], tile_no[:, :, :],
                                      tile_end[:, :].unsqueeze(1).to_broadcast([P, TILES, E]), ALU.is_ge))
                table(v.tensor_reduce(tile_e[:, :], passed[:, :, :], AX_X, ALU.add))
                table(v.tensor_scalar(w_off[:, :], tile_e[:, :], float(E - 1), float(F), ALU.min, ALU.mult))
                table(v.tensor_scalar(s_off[:, :], tile_e[:, :], float(E - 1), float(P), ALU.min, ALU.mult))
                table(v.tensor_tensor(jumps[:, :, :], passed[:, :, :],
                                      jump[:, :].unsqueeze(1).to_broadcast([P, TILES, E]), ALU.mult))
                table(v.tensor_reduce(tile_row[:, :], jumps[:, :, :], AX_X, ALU.add))
                v.scalar_tensor_tensor(row_off[:, :], tile_no[:, :, 0], float(P), tile_row[:, :],
                                       ALU.mult, ALU.add).then_inc(table_ready, 1)
                dve.wait_ge(ld_s1, 16)

                def ffn(i, k):
                    if a := ffn_tile(i, k, 1):
                        t, c, _ = a
                        dve.wait_ge(val_psum, t + 1)
                        dve.wait_ge(act_ready, t + 1)
                        if second_on(t):
                            dve.wait_ge(hidT_psum, t - 1)
                        v.tensor_tensor(hid[:, c % 2, :], bank[3 + c % 2][:, :], act_sb[:, c % 2, :],
                                        ALU.mult).then_inc(hid_ready, 1)
                    if a := ffn_tile(i, k, -1):
                        t, c, r = a
                        off = dve.value_load(s_off[0:1, bass.ds(t, 1)], min_val=0, max_val=(E - 1) * P)
                        dve.wait_ge(y_psum, t + 1)
                        v.scalar_tensor_tensor(yo[:, c % XB, :], bank[6][:, 0:P], xs[:, c % XB, P + 1:P + 2],
                                               s1_sb[:, bass.ds(off, P)], ALU.mult, ALU.mult).then_inc(yo_ready, 1)

                ffn_steps(dve, ffn)

                for g in range(NG):
                    dve.wait_ge(got_rows[g], 16)
                    two = got[:, g, :].rearrange("p (t k d) -> p t k d", t=G, k=TOP)
                    part = fin[:, g, 0:G * P].rearrange("p (t d) -> p t d", t=G)
                    v.tensor_tensor(part, two[:, :, 0, :], two[:, :, 1, :], ALU.add).then_inc(pair_sum, 1)
                    dve.wait_ge(pair_sum, g + 1)
                    at = x2[:, G * g:G * g + G, :]
                    v.tensor_tensor(at, at, part, ALU.add).then_inc(fin_ready, 1)


_INS = ['x', 'ctx_1024', 'L0_xattn_Wq', 'L0_xattn_bq', 'L0_xattn_Wk', 'L0_xattn_bk', 'L0_xattn_Wv', 'L0_xattn_bv',
        'L0_xattn_Wo', 'L0_xattn_bo', 'L0_ffn_router_w', 'L0_ffn_wv', 'L0_ffn_sv', 'L0_ffn_w', 'L0_ffn_s',
        'L0_ffn_w1', 'L0_ffn_s1']
_OUTS = [((16, 128, 128), 'float32')]


def kernel(**inputs):
    import numpy as _np
    import concourse.bacc as _bacc
    from concourse import mybir as _mybir
    from concourse.bass_utils import run_bass_kernel_spmd as _run

    nc = _bacc.Bacc("TRN2", target_bir_lowering=False, num_devices=1)
    arrays, args = {}, []
    for name in _INS:
        a = _np.ascontiguousarray(inputs[name])
        arrays[f"in_{name}_dram"] = a
        args.append(nc.dram_tensor(f"in_{name}_dram", a.shape, _mybir.dt.from_np(a.dtype), kind="ExternalInput").ap())
    for i, (shape, dtype) in enumerate(_OUTS):
        dt = _mybir.dt.from_np(_np.dtype(dtype))
        args.append(nc.dram_tensor(f"out_{i}_dram", shape, dt, kind="ExternalOutput").ap())
    xattn_moe_kernel(nc, *args)
    r = _run(nc, [arrays], core_ids=[0])
    got = tuple(r.results[0][f"out_{i}_dram"] for i in range(len(_OUTS)))
    return got[0]
```

```python
from contextlib import ExitStack

import concourse.bass as bass
from concourse import mybir

ALU = mybir.AluOpType
ACT = mybir.ActivationFunctionType
AX_X = mybir.AxisListType.X
F32 = mybir.dt.float32
I32 = mybir.dt.int32
U32 = mybir.dt.uint32
F32R = mybir.dt.float32r

P = 128
NT = 16
G = 4
NG = NT // G
H = 16
HD = 8
DK = 64
QW = (HD + 1) * H
E = 8
F = 512
FC = F // P
TOP = 2
ROWW = P + 2
TOKENS = NT * P
REGION = TOKENS + P
TILES = (TOP * TOKENS + E * (P - 1)) // P
SPARE = TOP * G
assert SPARE >= TILES - TOP * TOKENS // P
EARLY_G = NG // 2
EARLY = -(-(TOP * TOKENS * EARLY_G // NG - E * (P - 1)) // P)
LEFT = TILES - EARLY
ROWS = E * REGION + SPARE * P
NOWHERE = 1 << 20
XB = 12
EPS = 1e-5
SCALE = DK ** -0.5


def xattn_moe_kernel(nc, x, ctx, Wq, bq, Wk, bk, Wv, bv, Wo, bo, router_w, wv, sv, w, s, w1, s1, out):
    stack = ExitStack()
    with stack:
        def sb(name, shape, dt=F32):
            return stack.enter_context(nc.sbuf_tensor(name, shape, dt))

        def before_it(name, shape, dt):
            with nc.sbuf_tensor(name, shape, dt) as t:
                return t

        def sem(name):
            return stack.enter_context(nc.semaphore(name))

        bank = [stack.enter_context(nc.psum_tensor(f"bank{i}", [P, 512], F32)) for i in range(8)]

        routed = nc.dram_tensor("routed", [ROWS, ROWW], F32, kind="Internal").ap()
        expert_out = nc.dram_tensor("expert_out", [TOP * TOKENS, P], F32, kind="Internal").ap()

        ident = sb("ident", [P, P])
        ones = sb("ones", [P, P])
        before = sb("before", [P, P])
        head_mask = sb("head_mask", [P, H])
        minus_half = sb("minus_half", [P, NT])
        eps = sb("eps", [P, NT])
        pause_dve, pause_act = sb("pause_dve", [P, 2]), sb("pause_act", [P, 1])
        expert_no = sb("expert_no", [P, G, E])
        region0 = sb("region0", [P, G, E])
        tile_edges = sb("tile_edges", [P, E, NT])
        tile_no = sb("tile_no", [P, TILES, E])
        pad_rows = sb("pad_rows", [P, ROWW])

        q9 = sb("q9", [HD + 1, DK])
        k9 = sb("k9", [HD + 1, DK])
        v9 = sb("v9", [HD + 1, 2 * DK])
        qT = sb("qT", [DK, HD + 1])
        kT = sb("kT", [DK, HD + 1])
        vT = sb("vT", [P, HD + 1])
        qT_rep = sb("qT_rep", [DK, H, HD])
        bq_rep = sb("bq_rep", [DK, P])
        bv_col = sb("bv_col", [P, 1])
        wv_diag = sb("wv_diag", [P, HD * (P + H)])
        wo_sb = sb("wo_sb", [P, HD, P])
        bo_row = sb("bo_row", [1, P])
        out_bias = sb("out_bias", [1, P])
        q_proj = sb("q_proj", [P, HD + 1, H])
        q_bias = sb("q_bias", [P, HD + 1, H])
        o_proj = sb("o_proj", [P, P])
        router = sb("router", [P, E])

        x_sb = sb("x_sb", [P, NT, P])
        ctx_sb = sb("ctx_sb", [P, NT, P])
        ctx_ig = sb("ctx_ig", [P, NT, HD, H])
        stats = sb("stats", [P, NT, 6])
        mv = sb("mv", [P, NT, 2])
        rstd = sb("rstd", [P, NT])
        shift = sb("shift", [P, NT])
        vtmp = sb("vtmp", [P, NT])

        xn = sb("xn", [P, 2, P])
        xnT = sb("xnT", [P, 2, P])
        q_sb = sb("q_sb", [P, 2, HD + 1, H])
        qk = sb("qk", [P, 2, HD, H * H])
        neg_max = sb("neg_max", [P, 2, H])
        shifted = sb("shifted", [P, 2, H, H])
        xsT_parts = before_it("xsT_parts", [P, 2, 2, P], F32R)
        sums_in = sb("sums_in", [P, 2, P + H, H])
        rowinv = sb("rowinv", [P, 2, H])
        pv, probs = sums_in[:, :, 0:P, :], sums_in[:, :, P:P + H, :]
        z0 = sb("z0", [P, 2, P + H])
        z = sb("z", [P, 2, P])
        zT = sb("zT", [P, 2, P])

        stats2 = sb("stats2", [P, G, 6])
        mv2 = sb("mv2", [P, G, 2])
        vtmp2 = sb("vtmp2", [P, G])
        rstd2 = sb("rstd2", [P, G])
        shift2 = sb("shift2", [P, G])
        rows = sb("rows", [P, G, TOP, ROWW])
        dest = sb("dest", [P, NT, TOP])
        gates = sb("gates", [P, G, TOP])
        rows_i = rows[:, :, :, :].bitcast(I32)
        xn2 = sb("xn2", [P, G, P])
        xn2T = sb("xn2T", [P, G, P])
        top8 = sb("top8", [P, G, E])
        order = sb("order", [P, G, E], U32)
        r2 = sb("r2", [P, G, E + TOP])
        r3 = sb("r3", [P, G, E + TOP])
        r_sum = sb("r_sum", [P, G])
        r_inv = sb("r_inv", [P, G])
        pick = sb("pick", [P, TOP, G, E])
        picked = sb("picked", [P, G, E])
        group_sum = sb("group_sum", [P, E])
        carry = sb("carry", [P, E])
        slot = sb("slot", [P, G, E])
        slot_of = sb("slot_of", [P, TOP, G, E])
        place = sb("place", [P, TOP, G])
        pos = sb("pos", [P, TOP, G], I32)

        over = sb("over", [P, E, NT])
        n_tiles = sb("n_tiles", [P, E])
        tile_end = sb("tile_end", [P, E])
        jump = sb("jump", [P, E])
        passed = sb("passed", [P, TILES, E])
        jumps = sb("jumps", [P, TILES, E])
        tile_e = sb("tile_e", [P, TILES])
        tile_row = sb("tile_row", [P, TILES])
        w_off = sb("w_off", [P, TILES], I32)
        s_off = sb("s_off", [P, TILES], I32)
        row_off = sb("row_off", [P, TILES], I32)
        pad_off = sb("pad_off", [P, E], I32)

        early_end = sb("early_end", [P, 1 + E])
        early = sb("early", [P, E + 1])
        edges_left = sb("edges_left", [P, E, NT])
        jump_left = sb("jump_left", [P, E])
        left_no = sb("left_no", [P, LEFT])

        g_lo = before_it("g_lo", [P, E * F], F32R)
        g_sb = sb("g_sb", [P, E * F])
        v_lo = before_it("v_lo", [P, E * F], F32R)
        v_sb = sb("v_sb", [P, E * F])
        v_hi = before_it("v_hi", [P, E * F], F32R)
        g_scale = sb("g_scale", [P, E * F])
        g_hi = sb("g_hi", [P, E * F], F32R)
        w1_sb = sb("w1_sb", [P, E * F])
        xs = sb("xs", [P, XB, ROWW])
        yo = sb("yo", [P, XB, P])
        sv_rows = sb("sv_rows", [E * FC, P])
        sv_col = sb("sv_col", [P, E * FC])
        s1_sb = wo_sb[:, :, :].rearrange("p c n -> p (c n)")
        xsT_hi, xsT_lo = xsT_parts[:, 0, :, :], xsT_parts[:, 1, :, :]
        ctx_flat = ctx_sb[:, :, :].rearrange("p t n -> p (t n)")
        act_sb = ctx_flat[:, 0:2 * F].rearrange("p (b n) -> p b n", b=2)
        hid = ctx_flat[:, 2 * F:4 * F].rearrange("p (b n) -> p b n", b=2)
        ig_flat = ctx_ig[:, :, :, :].rearrange("p t i h -> p (t i h)")
        hidT = ig_flat[:, 0:2 * F].rearrange("p (b n) -> p b n", b=2)
        xs_i = xs[:, :, :].bitcast(I32)
        got = [sums_in[:, g // 2, (g % 2) * (P // 2):(g % 2 + 1) * (P // 2), :].rearrange("p m g -> p (m g)")
               for g in range(NG)]
        fin = qk[:, :, :, :].rearrange("p a (q i) s -> p (a q) (i s)", q=2)

        ld_small, ld_wo, ld_bo, ld_router, ld_sv = (sem(n) for n in (
            "ld_small", "ld_wo", "ld_bo", "ld_router", "ld_sv"))
        ld_x = [sem(f"ld_x{g}") for g in range(NG)]
        ld_ctx = [sem(f"ld_ctx{g}") for g in range(NG)]
        ld_wv, ld_wg, ld_gs, ld_w1, ld_s1 = (sem(n) for n in ("ld_wv", "ld_wg", "ld_gs", "ld_w1", "ld_s1"))
        pool_set = sem("pool_set")
        setup_pe, setup_dve, setup_step = sem("setup_pe"), sem("setup_dve"), sem("setup_step")
        ln1_mv, ln1_rstd, ln1_shift = sem("ln1_mv"), sem("ln1_rstd"), sem("ln1_shift")
        ln1_eps = sem("ln1_eps")
        ln1_stats = sem("ln1_stats")
        ctx_turned = sem("ctx_turned")
        xn_ready, xnT_psum, xnT_ready = sem("xn_ready"), sem("xnT_psum"), sem("xnT_ready")
        q_psum, q_ready, qk_ready = sem("q_psum"), sem("q_ready"), sem("qk_ready")
        s_psum, max_ready, s_shifted = sem("s_psum"), sem("max_ready"), sem("s_shifted")
        p_ready, inv_ready = sem("p_ready"), sem("inv_ready")
        pv_ready, z0_ready, z_ready = sem("pv_ready"), sem("z0_ready"), sem("z_ready")
        zT_psum, zT_ready, o_psum, x2_ready = (sem(n) for n in ("zT_psum", "zT_ready", "o_psum", "x2_ready"))
        sv_ready = sem("sv_ready")
        st2_ready, w1_scaled, g_scaled = sem("st2_ready"), sem("w1_scaled"), sem("g_scaled")
        g_hi_ready, v_hi_ready = sem("g_hi_ready"), sem("v_hi_ready")
        g_lo_ready, v_lo_ready = sem("g_lo_ready"), sem("v_lo_ready")
        mv2_ready, eps2_ready, rstd2_ready, shift2_ready = (
            sem(n) for n in ("mv2_ready", "eps2_ready", "rstd2_ready", "shift2_ready"))
        xn2_ready, carry_ready, meta_ready = sem("xn2_ready"), sem("carry_ready"), sem("meta_ready")
        rows_ready, xn2T_psum, xn2T_ready, logits_psum = (
            sem(n) for n in ("rows_ready", "xn2T_psum", "xn2T_ready", "logits_psum"))
        logits_shifted, logits_exp, picked_ready, gates_ready, rank_psum, pos_ready = (
            sem(n) for n in ("logits_shifted", "logits_exp", "picked_ready", "gates_ready", "rank_psum", "pos_ready"))
        route_step = sem("route_step")
        scattered = sem("scattered")
        counts_psum, counts_read, table_step, early_ready, pads_known, table_ready, padded = (
            sem(n) for n in ("counts_psum", "counts_read", "table_step", "early_ready", "pads_known", "table_ready", "padded"))
        xs_loaded = [sem(f"xs_loaded{b}") for b in range(XB)]
        y_sent = [sem(f"y_sent{b}") for b in range(XB)]
        xsT_psum, xsT_ready, gate_psum, val_psum = (
            sem(n) for n in ("xsT_psum", "xsT_ready", "gate_psum", "val_psum"))
        act_ready, hid_ready, hidT_psum, hidT_ready = (
            sem(n) for n in ("act_ready", "hid_ready", "hidT_psum", "hidT_ready"))
        xsT_lo_ready = sem("xsT_lo_ready")
        y_psum, yo_ready = sem("y_psum"), sem("yo_ready")
        got_rows = [sem(f"got_rows{g}") for g in range(NG)]
        pair_sum, fin_ready, stored = sem("pair_sum"), sem("fin_ready"), sem("stored")

        POOL_SET = 16
        HALF = E * F // 2
        SHARE = E * FC // (G * (NG - 2))
        AHEAD = 2
        NORM, LOGITS, PLACES = 7, 8, 9
        SENDS = {9: 2, 10: 3, 11: 3}
        assert sum(SENDS.values()) == G * TOP
        BETWEEN = (1, 0, 2, 1)

        def tile_at(g, j, lag):
            t = g * G + (AHEAD + j - lag)
            if isinstance(t, int) and not 0 <= t < NT:
                return None
            return t, (AHEAD + j - lag) % 2

        def group_at(g, j, lag):
            if (AHEAD + j - lag) % G:
                return None
            n = g + (AHEAD + j - lag) // G
            return None if isinstance(n, int) and not 0 <= n < NG else (n,)

        def second_on(t):
            return not isinstance(t, int) or t >= 2

        def first_on(t):
            return not isinstance(t, int) or t >= 1

        def attention_steps(eng, step):
            for g in (-1, 0):
                for j in range(G):
                    step(g, j)
            with eng.Fori(1, NG - 1) as g:
                for j in range(G):
                    step(g, j)

        SENT = 16 * G * TOP
        full = (TILES - 3) // XB
        assert TILES - 3 == full * XB

        FIRST = EARLY - 3
        assert FIRST < XB

        def last_steps(step, ffn, table):
            for j in range(G):
                step(NG - 1, j)
            done = -3
            for j, many in enumerate(BETWEEN):
                for k in range(done, done + many):
                    ffn(0, k)
                done += many
                step(NG, j)
            table()
            for k in range(done, FIRST):
                ffn(0, k)

        def ffn_steps(eng, ffn):
            for k in range(FIRST, XB):
                ffn(0, k)
            with eng.Fori(1, full) as i:
                for k in range(XB):
                    ffn(i, k)
            for k in range(3):
                ffn(full, k)

        def ffn_tile(i, k, ahead):
            c = 1 + k + ahead
            if isinstance(i, int) and not 0 <= i * XB + c < TILES:
                return None
            return i * XB + c, c, i

        def uses(i, c):
            return i + (c // XB + 1)

        with nc.Block() as block:

            @block.sync
            def _(sp):
                for g in range(NG):
                    at = slice(g * G, g * G + G)
                    sp.dma_start(x_sb[:, at, :], x.rearrange("t p d -> p t d")[:, at, :]).then_inc(ld_x[g], 16)
                    sp.dma_start(ctx_sb[:, at, :], ctx.rearrange("t p d -> p t d")[:, at, :]).then_inc(ld_ctx[g], 16)
                sp.wait_ge(ld_ctx[NG - 1], 16)
                sp.dma_start(g_sb[:, :].rearrange("p (e f) -> p e f", e=E), w.rearrange("e d f -> d e f")).then_inc(ld_wg, 16)
                sp.dma_start(g_scale[:, :], s.rearrange("e a f -> (e a f)").partition_broadcast(P)).then_inc(ld_gs, 16)
                sp.dma_start(w1_sb[:, :].rearrange("p (e c n) -> p e c n", e=E, c=FC),
                             w1.rearrange("e (c p) n -> p e c n", p=P)).then_inc(ld_w1, 16)
                sp.dma_start(v_sb[:, :].rearrange("p (e f) -> p e f", e=E), wv.rearrange("e d f -> d e f")).then_inc(ld_wv, 16)
                sp.wait_ge(setup_pe, 3)
                sp.dma_start(s1_sb[:, :], s1.rearrange("e a n -> (e a n)").partition_broadcast(P)).then_inc(ld_s1, 16)


                def load(i, c):
                    if not (isinstance(i, int) and i == 0):
                        sp.wait_ge(y_sent[c], 16 * i)
                    r0 = sp.value_load(row_off[0:1, bass.ds(i * XB + c, 1)], min_val=0, max_val=ROWS - P)
                    sp.dma_start(xs[:, c, :], routed[bass.ds(r0, P), :]).then_inc(xs_loaded[c], 16)

                sp.wait_ge(early_ready, 1)
                sp.wait_ge(scattered, SENT * (EARLY_G + 1))
                for c in range(EARLY):
                    load(0, c)
                sp.wait_ge(pads_known, 1)
                for e in range(E):
                    r0 = sp.value_load(pad_off[0:1, e:e + 1], min_val=0, max_val=ROWS - P)
                    sp.dma_start(routed[bass.ds(r0, P), :], pad_rows[:, :]).then_inc(padded, 16)
                sp.wait_ge(table_ready, 1)
                sp.wait_ge(padded, 16 * E)
                sp.wait_ge(scattered, SENT * (NG + 1))
                whole = TILES // XB
                for c in range(EARLY, XB):
                    load(0, c)
                with sp.Fori(1, whole) as i:
                    for c in range(XB):
                        load(i, c)
                for c in range(TILES - whole * XB):
                    load(whole, c)

                for b in range(XB):
                    sp.wait_ge(y_sent[b], 16 * len(range(b, TILES, XB)))
                pairs = expert_out.rearrange("(t p k) d -> p t (k d)", p=P, k=TOP)
                out_rows = out.rearrange("t p d -> p t d")
                for g in range(NG):
                    at = slice(G * g, G * g + G)
                    sp.dma_start(got[g].rearrange("p (t n) -> p t n", t=G), pairs[:, at, :]).then_inc(got_rows[g], 16)
                for g in range(NG):
                    at = slice(G * g, G * g + G)
                    sp.wait_ge(fin_ready, g + 1)
                    sp.dma_start(out_rows[:, at, :], x_sb[:, at, :]).then_inc(stored, 16)
                sp.wait_ge(stored, 16 * NG)

            @block.gpsimd
            def _(pool):
                last_row, last_dest = pool.to_reg(ROWS - 1), pool.to_reg(TOP * TOKENS - 1)
                steps = [0]

                def built(ins):
                    steps[0] += 1
                    ins.then_inc(pool_set, 1)
                    pool.wait_ge(pool_set, steps[0])

                built(pool.memset(ident[:, :], 0.0))
                built(pool.affine_select(out=ident[:, :], in_=ident[:, :], compare_op=ALU.not_equal, fill=1.0,
                                         base=0, pattern=[[-1, P]], channel_multiplier=1))
                built(pool.memset(head_mask[:, :], SCALE))
                built(pool.affine_select(out=head_mask[:, :], in_=head_mask[:, :], compare_op=ALU.is_ge, fill=0.0,
                                         base=0, pattern=[[-HD, H]], channel_multiplier=1))
                built(pool.affine_select(out=head_mask[:, :], in_=head_mask[:, :], compare_op=ALU.is_ge, fill=0.0,
                                         base=HD - 1, pattern=[[HD, H]], channel_multiplier=-1))
                built(pool.memset(minus_half[:, :], -0.5))
                built(pool.memset(eps[:, :], EPS))
                built(pool.memset(ones[:, :], 1.0))
                built(pool.affine_select(out=before[:, :], in_=ones[:, :], compare_op=ALU.is_ge, fill=0.0,
                                         base=-1, pattern=[[1, P]], channel_multiplier=-1))
                built(pool.iota(expert_no[:, :, :], pattern=[[0, G], [1, E]], base=0, channel_multiplier=0,
                                allow_small_or_imprecise_dtypes=True))
                built(pool.iota(region0[:, :, :], pattern=[[0, G], [REGION, E]], base=0, channel_multiplier=0,
                                allow_small_or_imprecise_dtypes=True))
                built(pool.iota(dest[:, :, :], pattern=[[TOP * P, NT], [1, TOP]], base=0, channel_multiplier=TOP,
                                allow_small_or_imprecise_dtypes=True))
                built(pool.iota(tile_edges[:, :, :], pattern=[[0, E], [P, NT]], base=0, channel_multiplier=0,
                                allow_small_or_imprecise_dtypes=True))
                built(pool.iota(tile_no[:, :, :], pattern=[[1, TILES], [0, E]], base=0, channel_multiplier=0,
                                allow_small_or_imprecise_dtypes=True))
                built(pool.memset(pad_rows[:, :], 0.0))
                built(pool.iota(pad_rows[:, P:P + 1].bitcast(I32), pattern=[[0, 1]], base=NOWHERE, channel_multiplier=0))
                assert steps[0] == POOL_SET
                assert 16 * SPARE == SENT and SPARE == 2 * G

                def spare_tile(n):
                    r0 = E * REGION + n * P
                    pool.dma_start(routed[r0:r0 + P, :], pad_rows[:, :]).then_inc(scattered, 16)

                for g in range(NG):
                    at = slice(g * G, g * G + G)
                    pool.wait_ge(ln1_mv, g * G + G)
                    pool.tensor_tensor(vtmp[:, at], mv[:, at, 1], eps[:, at], ALU.add).then_inc(ln1_eps, 1)
                    pool.wait_ge(ln1_eps, g + 1)
                    pool.tensor_tensor(rstd[:, at], vtmp[:, at], minus_half[:, at], ALU.pow).then_inc(ln1_rstd, 1)

                def step(g, j):
                    if a := tile_at(g, j, 1):
                        t, b = a
                        if isinstance(t, int) and t == 0:
                            pool.wait_ge(ctx_turned, NG)
                        pool.wait_ge(p_ready, t + 1)
                        if second_on(t):
                            pool.wait_ge(z0_ready, t - 1)
                        pool.tensor_tensor(
                            pv[:, b, :, :].rearrange("p (h i) g -> p h i g", h=H),
                            probs[:, b, :, :].unsqueeze(2).to_broadcast([P, H, HD, H]),
                            ctx_ig[:, t, :, :].unsqueeze(1).to_broadcast([P, H, HD, H]), ALU.mult).then_inc(pv_ready, 1)
                    a = group_at(g, j, NORM - 1)
                    if last := group_at(g, j, NORM - 2):
                        a = last if last[0] == NG - 1 else a
                    if a and (a == last or a[0] < NG - 1):
                        n, = a
                        pool.wait_ge(mv2_ready, n * G + G)
                        pool.tensor_tensor(vtmp2[:, :], mv2[:, :, 1], eps[:, 0:G], ALU.add).then_inc(eps2_ready, 1)
                        pool.wait_ge(eps2_ready, n + 1)
                        pool.tensor_tensor(rstd2[:, :], vtmp2[:, :], minus_half[:, 0:G], ALU.pow).then_inc(rstd2_ready, 1)
                    if isinstance(g, int) and g <= 0:
                        spare_tile((g + 1) * G + j)
                    sent = 0
                    for lag, many in SENDS.items():
                        if a := group_at(g, j, lag):
                            n, = a
                            if sent == 0:
                                pool.wait_ge(rows_ready, (n + 2) * TOP)
                                pool.wait_ge(meta_ready, (n + 1) * 2)
                                pool.wait_ge(pos_ready, n + 2)
                            for m in range(sent, sent + many):
                                pool.indirect_dma_start(
                                    out=routed[:, :],
                                    out_offset=bass.IndirectOffsetOnAxis(ap=pos[:, m % TOP, m // TOP:m // TOP + 1], axis=0),
                                    in_=rows[:, m // TOP, m % TOP, :], in_offset=None,
                                    bounds_check=last_row).then_inc(scattered, 16)
                        sent += many

                for t in range(-AHEAD, NT + max(SENDS)):
                    step((t - AHEAD) // G, (t - AHEAD) % G)

                for t in range(TILES):
                    pool.wait_ge(yo_ready, t + 1)
                    pool.indirect_dma_start(
                        out=expert_out[:, :],
                        out_offset=bass.IndirectOffsetOnAxis(ap=xs_i[:, t % XB, P:P + 1], axis=0),
                        in_=yo[:, t % XB, :], in_offset=None,
                        bounds_check=last_dest, oob_is_err=False).then_inc(y_sent[t % XB], 16)

            @block.scalar
            def _(act):
                act.sem_inc(xn2T_ready, 1)
                act.sem_inc(rows_ready, TOP)
                twice = lambda w: w.unsqueeze(1).to_broadcast([w.shape[0], 2, DK])
                for to, frm in ((q9[0:HD, :], Wq), (q9[HD:HD + 1, :], bq.unsqueeze(0)),
                                (k9[0:HD, :], Wk), (k9[HD:HD + 1, :], bk.unsqueeze(0)),
                                (v9[0:HD, :].rearrange("p (a v) -> p a v", a=2), twice(Wv)),
                                (v9[HD:HD + 1, :].rearrange("p (a v) -> p a v", a=2), twice(bv.unsqueeze(0)))):
                    act.dma_start(to, frm).then_inc(ld_small, 16)
                act.dma_start(wo_sb[:, :, :], Wo.rearrange("(c p) n -> p c n", p=P)).then_inc(ld_wo, 16)
                act.dma_start(bo_row[:, :], bo.unsqueeze(0)).then_inc(ld_bo, 16)
                act.dma_start(sv_rows[:, :], sv.rearrange("e a (c p) -> (e a c) p", p=P)).then_inc(ld_sv, 16)
                act.dma_start(router[:, :], router_w).then_inc(ld_router, 16)

                def turn(g):
                    at = slice(g * G, g * G + G)
                    act.wait_ge(ld_ctx[g], 16)
                    nc.scalar.copy(ctx_ig[:, at, :, :],
                                   ctx_sb[:, at, :].rearrange("p t (h i) -> p t i h", h=H)).then_inc(ctx_turned, 1)

                turn(0)

                def step(g, j):
                    if a := tile_at(g, j, -2):
                        t, b = a
                        if isinstance(t, int) and t % G == 0:
                            act.wait_ge(ln1_shift, t // G + 1)
                        if second_on(t):
                            act.wait_ge(xnT_psum, t - 1)
                        nc.scalar.activation(xn[:, b, :], x_sb[:, t, :], ACT.Identity, scale=rstd[:, bass.ds(t, 1)],
                                             bias=shift[:, bass.ds(t, 1)]).then_inc(xn_ready, 1)
                    if a := tile_at(g, j, -1):
                        t, b = a
                        act.wait_ge(q_psum, t + 1)
                        if second_on(t):
                            act.wait_ge(s_psum, t - 1)
                        nc.scalar.copy(q_sb[:, b, :, :].rearrange("p i h -> p (i h)"), bank[1][:, 0:QW]).then_inc(q_ready, 1)
                    if isinstance(g, int) and g == -1 and j > 0:
                        turn(j)
                    if a := tile_at(g, j, 1):
                        t, b = a
                        act.wait_ge(s_shifted, t + 1)
                        if second_on(t):
                            act.wait_ge(z0_ready, t - 1)
                        nc.scalar.activation(probs[:, b, :, :], shifted[:, b, :, :], ACT.Exp).then_inc(p_ready, 1)
                    if a := group_at(g, j, NORM):
                        n, = a
                        act.wait_ge(shift2_ready, n + 1)
                        act.wait_ge(rows_ready, (n + 1) * TOP)
                        act.wait_ge(xn2T_psum, n + 1)
                        for m in range(G):
                            t = n * G + m
                            nc.scalar.activation(xn2[:, m, :], x_sb[:, t, :], ACT.Identity, scale=rstd2[:, m:m + 1],
                                                 bias=shift2[:, m:m + 1]).then_inc(xn2_ready, 1)
                    if a := group_at(g, j, LOGITS):
                        n, = a
                        act.wait_ge(logits_shifted, n + 1)
                        nc.scalar.activation(r3[:, :, :], r2[:, :, :], ACT.Exp).then_inc(logits_exp, 1)
                    if isinstance(g, int) and (g, j) == (NG - 1, AHEAD):
                        nc.scalar.activation(pause_act[:, :], eps[:, 0:1], ACT.Gelu_apprx_tanh)
                    if isinstance(g, int) and (g, j) in ((-1, 3), (0, 0)):
                        half = slice(0, HALF) if g < 0 else slice(HALF, 2 * HALF)
                        act.wait_ge(g_scaled, 1 if g < 0 else 2)
                        nc.scalar.copy(g_hi[:, half], g_sb[:, half]).then_inc(g_hi_ready, 1)
                    if not isinstance(g, int):
                        share = (g - 1) * (G * SHARE) + j * SHARE
                        for c in range(SHARE):
                            chunk = w1_sb[:, bass.ds((share + c) * P, P)]
                            nc.scalar.activation(chunk, chunk, ACT.Copy, scale=sv_col[:, bass.ds(share + c, 1)]).then_inc(w1_scaled, 1)
                        at = bass.ds(share * P, SHARE * P)
                        nc.scalar.copy(v_hi[:, at], v_sb[:, at]).then_inc(v_hi_ready, 1)
                    elif (g, j) == (0, G - 1):
                        act.wait_ge(ld_w1, 16)
                        act.wait_ge(sv_ready, 1)
                        act.wait_ge(ld_wv, 16)
                        act.wait_ge(g_scaled, 2)
                    if a := tile_at(g, j, -2):
                        t, b = a
                        act.wait_ge(xnT_psum, t + 1)
                        if second_on(t):
                            act.wait_ge(q_psum, t - 1)
                        nc.scalar.copy(xnT[:, b, :], bank[0][:, 0:P]).then_inc(xnT_ready, 1)
                    if a := tile_at(g, j, 2):
                        t, b = a
                        act.wait_ge(zT_psum, t + 1)
                        if second_on(t):
                            act.wait_ge(o_psum, t - 1)
                        nc.scalar.copy(zT[:, b, :], bank[4][:, 0:P]).then_inc(zT_ready, 1)
                    if a := tile_at(g, j, 2):
                        t, b = a
                        act.wait_ge(o_psum, t + 1)
                        nc.scalar.copy(x_sb[:, t, :], bank[5][:, 0:P]).then_inc(x2_ready, 1)
                    if a := group_at(g, j, NORM):
                        n, = a
                        act.wait_ge(xn2T_psum, n + 2)
                        act.wait_ge(logits_psum, n + 1)
                        nc.scalar.copy(xn2T[:, :, :].rearrange("p t n -> p (t n)"), bank[6][:, :]).then_inc(xn2T_ready, 1)
                    if a := group_at(g, j, PLACES):
                        n, = a
                        act.wait_ge(xn2_ready, n * G + G)
                        act.wait_ge(scattered, (n + 1) * SENT)
                        for k in range(TOP):
                            nc.scalar.copy(rows[:, :, k, 0:P], xn2[:, :, :]).then_inc(rows_ready, 1)
                        nc.scalar.copy(rows_i[:, :, :, P], dest[:, bass.ds(n * G, G), :]).then_inc(meta_ready, 1)
                        act.wait_ge(gates_ready, n + 1)
                        nc.scalar.copy(rows[:, :, :, P + 1], gates[:, :, :]).then_inc(meta_ready, 1)
                def ffn(i, k):
                    if a := ffn_tile(i, k, 2):
                        t, c, _ = a
                        act.wait_ge(xsT_psum, t + 1)
                        if second_on(t):
                            act.wait_ge(val_psum, t - 1)
                        nc.scalar.copy(xsT_hi[:, c % 2, :], bank[0][:, 0:P]).then_inc(xsT_ready, 1)
                    if a := ffn_tile(i, k, 1):
                        t, c, _ = a
                        act.wait_ge(gate_psum, t + 1)
                        if second_on(t):
                            act.wait_ge(hid_ready, t - 1)
                        nc.scalar.activation(act_sb[:, c % 2, :], bank[1 + c % 2][:, :],
                                             ACT.Gelu_apprx_tanh).then_inc(act_ready, 1)
                    if a := ffn_tile(i, k, 0):
                        t, c, _ = a
                        act.wait_ge(hidT_psum, t + 1)
                        if second_on(t):
                            act.wait_ge(y_psum, t - 1)
                        nc.scalar.copy(hidT[:, c % 2, :], bank[5][:, :]).then_inc(hidT_ready, 1)

                attention_steps(act, step)
                last_steps(step, ffn, lambda: None)
                ffn_steps(act, ffn)

            @block.tensor
            def _(pe):
                pe.sem_inc(logits_psum, 1)
                pe.sem_inc(xn2T_psum, 1)
                pe.wait_ge(pool_set, 2)
                pe.wait_ge(ld_small, 16 * 6)
                nc.tensor.transpose(bank[0][0:DK, 0:HD + 1], q9[:, :], ident[0:HD + 1, 0:HD + 1])
                nc.tensor.transpose(bank[0][0:DK, 16:17 + HD], k9[:, :], ident[0:HD + 1, 0:HD + 1])
                nc.tensor.transpose(bank[0][:, 32:33 + HD], v9[:, :], ident[0:HD + 1, 0:HD + 1]).then_inc(setup_pe, 1)
                pe.wait_ge(setup_dve, 1)
                nc.tensor.matmul(bank[1][:, 0:HD + 1], qT_rep[:, :, :].rearrange("p h i -> p (h i)"), kT[:, :],
                                 start=True, stop=True)
                nc.tensor.matmul(bank[1][:, 16:17 + HD], bq_rep[:, :], kT[:, :], start=True, stop=True).then_inc(setup_pe, 1)
                pe.wait_ge(setup_dve, 2)
                pe.wait_ge(ld_sv, 16)
                nc.tensor.transpose(bank[6][:, 0:E * FC], sv_rows[:, :], ident[0:E * FC, 0:E * FC])
                pe.wait_ge(ld_wo, 16)
                for c in range(HD):
                    nc.tensor.matmul(bank[4][:, 0:P], wv_diag[:, c * P:c * P + P], wo_sb[:, c, :],
                                     start=(c == 0), stop=(c == HD - 1))
                for c in range(HD):
                    mm = nc.tensor.matmul(bank[5][0:1, 0:P], bv_col[:, :], wo_sb[:, c, :],
                                          start=(c == 0), stop=(c == HD - 1))
                mm.then_inc(setup_pe, 1)
                pe.wait_ge(setup_dve, 4)

                def step(g, j):
                    if a := tile_at(g, j, -1):
                        t, b = a
                        pe.wait_ge(xnT_ready, t + 1)
                        if first_on(t):
                            pe.wait_ge(q_ready, t)
                        nc.tensor.matmul(bank[1][:, 0:QW], xnT[:, b, :], q_proj[:, :, :].rearrange("p i h -> p (i h)"),
                                         start=True, stop=False)
                        nc.tensor.matmul(bank[1][:, 0:QW], ident[:, :], q_bias[:, :, :].rearrange("p i h -> p (i h)"),
                                         start=False, stop=True).then_inc(q_psum, 1)
                    if isinstance(g, int) and (g, j) == (0, 0):
                        pe.wait_ge(sv_ready, 1)
                    if a := group_at(g, j, LOGITS):
                        n, = a
                        pe.wait_ge(xn2T_ready, n + 2)
                        pe.wait_ge(pos_ready, n + 1)
                        if isinstance(n, int) and n == EARLY_G:
                            pe.wait_ge(counts_read, 1)
                        for m in range(G):
                            mm = nc.tensor.matmul(bank[7][:, m * E:m * E + E], xn2T[:, m, :], router[:, :],
                                                  start=True, stop=True)
                        mm.then_inc(logits_psum, 1)
                    if a := tile_at(g, j, 0):
                        t, b = a
                        pe.wait_ge(qk_ready, t + 1)
                        if second_on(t):
                            pe.wait_ge(s_shifted, t - 1)
                        nc.tensor.matmul(bank[2 + b][:, 0:H * H], ident[:, :],
                                         q_sb[:, b, HD, :].unsqueeze(2).to_broadcast([P, H, H]), start=True, stop=False)
                        for i in range(HD):
                            mm = nc.tensor.matmul(bank[2 + b][:, 0:H * H], ident[:, :], qk[:, b, i, :],
                                                  start=False, stop=(i == HD - 1))
                        mm.then_inc(s_psum, 1)
                    if a := tile_at(g, j, -2):
                        t, b = a
                        pe.wait_ge(xn_ready, t + 1)
                        if first_on(t):
                            pe.wait_ge(xnT_ready, t)
                        nc.tensor.transpose(bank[0][:, 0:P], xn[:, b, :], ident[:, :]).then_inc(xnT_psum, 1)
                    if a := group_at(g, j, LOGITS):
                        n, = a
                        pe.wait_ge(picked_ready, n + 1)
                        rank = bank[7][:, 64:64 + G * E]
                        flat = picked[:, :, :].rearrange("p t e -> p (t e)")
                        nc.tensor.matmul(rank, before[:, :], flat, start=True, stop=False)
                        for m in range(1, G):
                            nc.tensor.matmul(rank[:, m * E:], ones[:, :], flat[:, 0:(G - m) * E], start=False, stop=False)
                        nc.tensor.matmul(rank, ones[:, :], carry[:, :].unsqueeze(1).to_broadcast([P, G, E]),
                                         start=False, stop=True).then_inc(rank_psum, 1)
                    if a := tile_at(g, j, 2):
                        t, b = a
                        pe.wait_ge(z_ready, t + 1)
                        if first_on(t):
                            pe.wait_ge(zT_ready, t)
                        nc.tensor.transpose(bank[4][:, 0:P], z[:, b, :], ident[:, :]).then_inc(zT_psum, 1)
                    if a := tile_at(g, j, 2):
                        t, b = a
                        pe.wait_ge(zT_ready, t + 1)
                        if first_on(t):
                            pe.wait_ge(x2_ready, t)
                        nc.tensor.matmul(bank[5][:, 0:P], zT[:, b, :], o_proj[:, :], start=True, stop=False)
                        nc.tensor.matmul(bank[5][:, 0:P], ones[0:1, :], out_bias[:, :], start=False, stop=False)
                        nc.tensor.matmul(bank[5][:, 0:P], ident[:, :], x_sb[:, t, :], start=False, stop=True).then_inc(o_psum, 1)
                    if a := group_at(g, j, NORM):
                        n, = a
                        pe.wait_ge(xn2T_ready, n + 1)
                        for m in range(G):
                            pe.wait_ge(xn2_ready, n * G + (m + 1))
                            mm = nc.tensor.transpose(bank[6][:, m * P:m * P + P], xn2[:, m, :], ident[:, :])
                        mm.then_inc(xn2T_psum, 1)
                    if isinstance(g, int) and (g, j) == (NG - 1, 0):
                        counts(EARLY_G)

                def counts(groups):
                    pe.wait_ge(carry_ready, groups)
                    nc.tensor.matmul(bank[7][:, 128:128 + E], ones[:, :], carry[:, :], start=True, stop=True).then_inc(counts_psum, 1)

                def ffn(i, k):
                    if a := ffn_tile(i, k, 2):
                        t, c, r = a
                        pe.wait_ge(xs_loaded[c % XB], uses(r, c) * 16)
                        if first_on(t):
                            pe.wait_ge(xsT_lo_ready, t)
                        nc.tensor.transpose(bank[0][:, 0:P], xs[:, c % XB, 0:P], ident[:, :]).then_inc(xsT_psum, 1)
                    if a := ffn_tile(i, k, 1):
                        t, c, _ = a
                        if isinstance(t, int) and t == 0:
                            pe.wait_ge(early_ready, 1)
                            pe.wait_ge(g_lo_ready, 2)
                            pe.wait_ge(v_lo_ready, 2)
                            pe.wait_ge(w1_scaled, E * FC)
                        if isinstance(t, int) and t == EARLY:
                            pe.wait_ge(table_ready, 1)
                        off = pe.value_load(w_off[0:1, bass.ds(t, 1)], min_val=0, max_val=(E - 1) * F)
                        at = bass.ds(off, F)
                        pe.wait_ge(xsT_lo_ready, t + 1)
                        if second_on(t):
                            pe.wait_ge(hid_ready, t - 1)
                        for psum, hi, lo, ready in ((bank[1 + c % 2], g_hi, g_lo, gate_psum),
                                                    (bank[3 + c % 2], v_hi, v_lo, val_psum)):
                            nc.tensor.matmul(psum[:, :], xsT_hi[:, c % 2, :], hi[:, at], start=True, stop=False)
                            nc.tensor.matmul(psum[:, :], xsT_hi[:, c % 2, :], lo[:, at], start=False, stop=False)
                            nc.tensor.matmul(psum[:, :], xsT_lo[:, c % 2, :], hi[:, at], start=False, stop=True).then_inc(ready, 1)
                    if a := ffn_tile(i, k, -1):
                        t, c, _ = a
                        off = pe.value_load(w_off[0:1, bass.ds(t, 1)], min_val=0, max_val=(E - 1) * F)
                        pe.wait_ge(hidT_ready, t + 1)
                        if first_on(t):
                            pe.wait_ge(yo_ready, t)
                        for n in range(FC):
                            mm = nc.tensor.matmul(bank[6][:, 0:P], hidT[:, c % 2, n * P:n * P + P],
                                                  w1_sb[:, bass.ds(off + n * P, P)], start=(n == 0), stop=(n == FC - 1))
                        mm.then_inc(y_psum, 1)
                    if a := ffn_tile(i, k, 0):
                        t, c, _ = a
                        pe.wait_ge(hid_ready, t + 1)
                        if isinstance(t, int) and t == 0:
                            pe.wait_ge(x2_ready, NT)
                        else:
                            pe.wait_ge(hidT_ready, t)
                        for n in range(FC):
                            mm = nc.tensor.transpose(bank[5][:, n * P:n * P + P], hid[:, c % 2, n * P:n * P + P], ident[:, :])
                        mm.then_inc(hidT_psum, 1)

                pe.wait_ge(ld_router, 16)
                attention_steps(pe, step)
                last_steps(step, ffn, lambda: counts(NG))
                ffn_steps(pe, ffn)

            @block.vector
            def _(dve):
                v = nc.vector
                chain = [0]

                def small(ins):
                    chain[0] += 1
                    ins.then_inc(setup_step, 1)
                    dve.wait_ge(setup_step, chain[0])

                dve.sem_inc(pos_ready, 1)
                small(v.memset(wv_diag[:, :], 0.0))
                small(v.memset(carry[:, :], 0.0))
                small(v.memset(early_end[:, 0:1], 0.0))
                small(v.memset(early[:, E:], 0.0))
                dve.wait_ge(setup_pe, 1)
                small(v.tensor_copy(qT_rep[:, :, :], bank[0][0:DK, 0:HD].unsqueeze(1).to_broadcast([DK, H, HD])))
                small(v.tensor_copy(bq_rep[:, :], bank[0][0:DK, HD:HD + 1].to_broadcast([DK, P])))
                v.tensor_copy(kT[:, :], bank[0][0:DK, 16:17 + HD]).then_inc(setup_dve, 1)
                small(v.tensor_copy(bv_col[:, :], bank[0][:, 32 + HD:33 + HD]))
                for a in range(2):
                    at = slice(a * DK, a * DK + DK)
                    ins = v.tensor_copy(wv_diag[at, :].rearrange("p (c k) -> p c k", c=HD)[:, :, a * HD:a * HD + HD],
                                        bank[0][at, 32:32 + HD].unsqueeze(1).to_broadcast([DK, HD, HD]))
                    if a == 0:
                        small(ins)
                ins.then_inc(setup_dve, 1)

                def statistics(g):
                    dve.wait_ge(ld_x[g], 16)
                    for t in range(g * G, g * G + G):
                        v.bn_stats(stats[:, t, :], x_sb[:, t, :]).then_inc(ln1_stats, 1)
                    for t in range(g * G, g * G + G):
                        dve.wait_ge(ln1_stats, t + 1)
                        v.bn_aggr(mv[:, t, :], stats[:, t, :]).then_inc(ln1_mv, 1)

                def shifts(g):
                    at = slice(g * G, g * G + G)
                    dve.wait_ge(ln1_rstd, g + 1)
                    dve.wait_ge(ln1_mv, g * G + G)
                    v.scalar_tensor_tensor(shift[:, at], mv[:, at, 0], -1.0, rstd[:, at], ALU.mult, ALU.mult).then_inc(ln1_shift, 1)

                statistics(0)
                dve.wait_ge(setup_pe, 2)
                dve.wait_ge(pool_set, POOL_SET)
                v.tensor_tensor(q_proj[:, :, :], bank[1][:, 0:HD + 1].unsqueeze(2).to_broadcast([P, HD + 1, H]),
                                head_mask[:, :].unsqueeze(1).to_broadcast([P, HD + 1, H]), ALU.mult).then_inc(setup_dve, 1)
                v.tensor_scalar(q_bias[:, :, :], bank[1][:, 16:17 + HD].unsqueeze(2).to_broadcast([P, HD + 1, H]),
                                SCALE, None, ALU.mult).then_inc(setup_dve, 1)
                shifts(0)
                statistics(1)
                statistics(2)
                statistics(3)
                for g in range(1, NG):
                    shifts(g)

                def output_projection():
                    dve.wait_ge(setup_pe, 3)
                    dve.wait_ge(ld_bo, 16)
                    v.tensor_tensor(out_bias[:, :], bank[5][0:1, 0:P], bo_row[:, :], ALU.add)
                    v.tensor_copy(o_proj[:, :], bank[4][:, 0:P])
                    v.tensor_copy(sv_col[:, :], bank[6][:, 0:E * FC]).then_inc(sv_ready, 1)

                CHAIN = 13

                def step(g, j):
                    def wide(x):
                        return x.unsqueeze(2).to_broadcast

                    def normalised():
                        out_of, stats_of = tile_at(g, j, 2), tile_at(g, j, 3)
                        m = (AHEAD + j - 3) % G
                        if out_of:
                            t, b = out_of
                            dve.wait_ge(pv_ready, t + 1)
                            v.tensor_reduce(z0[:, b, :], sums_in[:, b, :, :], AX_X, ALU.add).then_inc(z0_ready, 1)
                        if stats_of:
                            t, b = stats_of
                            dve.wait_ge(x2_ready, t + 1)
                            v.bn_stats(stats2[:, m, :], x_sb[:, t, :]).then_inc(st2_ready, 1)
                        if out_of:
                            t, b = out_of
                            dve.wait_ge(z0_ready, t + 1)
                            v.reciprocal(rowinv[:, b, :], z0[:, b, P:P + H]).then_inc(inv_ready, 1)
                        if stats_of:
                            t, b = stats_of
                            dve.wait_ge(st2_ready, t + 1)
                            v.memset(pause_dve[:, 0:1], 0.0)
                            v.bn_aggr(mv2[:, m, :], stats2[:, m, :]).then_inc(mv2_ready, 1)
                        if out_of:
                            t, b = out_of
                            dve.wait_ge(inv_ready, t + 1)
                            if second_on(t):
                                dve.wait_ge(zT_psum, t - 1)
                            v.tensor_tensor(z[:, b, :].rearrange("p (h i) -> p h i", h=H),
                                            z0[:, b, 0:P].rearrange("p (h i) -> p h i", h=H),
                                            rowinv[:, b, :].unsqueeze(2).to_broadcast([P, H, HD]), ALU.mult).then_inc(z_ready, 1)

                    if a := tile_at(g, j, 0):
                        t, b = a
                        if isinstance(t, int) and t in (0, G):
                            dve.wait_ge(ctx_turned, 1 if t == 0 else NG)
                        dve.wait_ge(q_ready, t + 1)
                        if second_on(t):
                            dve.wait_ge(s_psum, t - 1)
                        v.tensor_tensor(qk[:, b, :, :].rearrange("p i (h g) -> p i h g", h=H),
                                        q_sb[:, b, 0:HD, :].unsqueeze(3).to_broadcast([P, HD, H, H]),
                                        ctx_ig[:, t, :, :].unsqueeze(2).to_broadcast([P, HD, H, H]),
                                        ALU.mult).then_inc(qk_ready, 1)
                    if a := tile_at(g, j, 1):
                        t, b = a
                        if isinstance(t, int) and t == 0:
                            dve.wait_ge(ld_wg, 16)
                            dve.wait_ge(ld_gs, 16)
                            for half in (slice(0, HALF), slice(HALF, 2 * HALF)):
                                v.tensor_tensor(g_sb[:, half], g_sb[:, half], g_scale[:, half], ALU.mult).then_inc(g_scaled, 1)
                        dve.wait_ge(s_psum, t + 1)
                        scores = bank[2 + b][:, 0:H * H].rearrange("p (h g) -> p h g", h=H)
                        v.tensor_reduce(neg_max[:, b, :], scores, AX_X, ALU.max, negate=True).then_inc(max_ready, 1)
                    elif not group_at(g, j, NORM):
                        normalised()
                    if a := tile_at(g, j, 1):
                        t, b = a
                        dve.wait_ge(max_ready, t + 1)
                        if second_on(t):
                            dve.wait_ge(p_ready, t - 1)
                        v.tensor_tensor(shifted[:, b, :, :], scores,
                                        neg_max[:, b, :].unsqueeze(2).to_broadcast([P, H, H]), ALU.add).then_inc(s_shifted, 1)
                        if isinstance(t, int) and t == 0:
                            output_projection()
                        if isinstance(t, int) and t in (1, 2):
                            half = slice((t - 1) * HALF, t * HALF)
                            dve.wait_ge(g_hi_ready, t)
                            v.tensor_tensor(g_lo[:, half], g_sb[:, half], g_hi[:, half], ALU.subtract).then_inc(g_lo_ready, 1)
                        if isinstance(t, int) and t == NT - 2:
                            early_counts()
                            values_rest(0)
                        if isinstance(t, int) and t == NT - 1:
                            early_table()
                    if a := group_at(g, j, NORM):
                        n, = a
                        dve.wait_ge(rstd2_ready, n + 1)
                        v.scalar_tensor_tensor(shift2[:, :], mv2[:, :, 0], -1.0, rstd2[:, :],
                                               ALU.mult, ALU.mult).then_inc(shift2_ready, 1)
                        dve.wait_ge(shift2_ready, n + 1)
                    if a := group_at(g, j, LOGITS):
                        n, = a
                        logits = bank[7][:, 0:G * E].rearrange("p (t e) -> p t e", t=G)
                        dve.wait_ge(logits_psum, n + 2)
                        v.memset(pause_dve[:, 1:2], 0.0)
                        for m in range(G):
                            v.max(top8[:, m, :], logits[:, m, :]).then_inc(route_step, 1)
                        dve.wait_ge(route_step, n * CHAIN + 4)
                        v.tensor_tensor(r2[:, :, 0:E], logits, wide(top8[:, :, 0])([P, G, E]), ALU.subtract)
                        v.tensor_tensor(r2[:, :, E:], top8[:, :, 0:TOP], wide(top8[:, :, 0])([P, G, TOP]),
                                        ALU.subtract).then_inc(logits_shifted, 1)
                        for m in range(G):
                            v.max_index(order[:, m, :], top8[:, m, :], logits[:, m, :]).then_inc(route_step, 1)
                        dve.wait_ge(route_step, n * CHAIN + 8)
                        v.tensor_tensor(pick[:, :, :, :], expert_no[:, :, :].unsqueeze(1).to_broadcast([P, TOP, G, E]),
                                        order[:, :, 0:TOP].rearrange("p t k -> p k t").unsqueeze(3).to_broadcast([P, TOP, G, E]),
                                        ALU.is_equal).then_inc(route_step, 1)
                        dve.wait_ge(route_step, n * CHAIN + 9)
                        v.tensor_tensor(picked[:, :, :], pick[:, 0, :, :], pick[:, 1, :, :], ALU.add).then_inc(picked_ready, 1)
                    if a := group_at(g, j, PLACES):
                        n, = a
                        dve.wait_ge(scattered, (n + 1) * SENT)
                        dve.wait_ge(logits_exp, n + 1)
                        v.tensor_reduce(r_sum[:, :], r3[:, :, 0:E], AX_X, ALU.add)
                        dve.wait_ge(picked_ready, n + 1)
                        v.tensor_reduce(group_sum[:, :], picked[:, :, :].rearrange("p t e -> p e t"), AX_X, ALU.add)
                        dve.wait_ge(rank_psum, n + 1)
                        rank = bank[7][:, 64:64 + G * E].rearrange("p (t e) -> p t e", t=G)
                        v.tensor_tensor(slot[:, :, :], rank, region0[:, :, :], ALU.add).then_inc(route_step, 1)
                        dve.wait_ge(route_step, n * CHAIN + 10)
                        v.tensor_tensor(slot_of[:, :, :, :], pick[:, :, :, :],
                                        slot[:, :, :].unsqueeze(1).to_broadcast([P, TOP, G, E]), ALU.mult).then_inc(route_step, 1)
                        v.reciprocal(r_inv[:, :], r_sum[:, :]).then_inc(route_step, 1)
                        v.tensor_tensor(carry[:, :], carry[:, :], group_sum[:, :], ALU.add).then_inc(carry_ready, 1)
                        dve.wait_ge(route_step, n * CHAIN + 12)
                        v.tensor_reduce(place[:, :, :], slot_of[:, :, :, :], AX_X, ALU.add).then_inc(route_step, 1)
                        v.tensor_tensor(gates[:, :, :], r3[:, :, E:], wide(r_inv[:, :])([P, G, TOP]), ALU.mult).then_inc(gates_ready, 1)
                        dve.wait_ge(route_step, n * CHAIN + 13)
                        v.tensor_copy(pos[:, :, :], place[:, :, :]).then_inc(pos_ready, 1)
                        dve.wait_ge(carry_ready, n + 1)
                    if tile_at(g, j, 1) or group_at(g, j, NORM):
                        normalised()
                    if isinstance(g, int) and (g, j) == (NG - 1, AHEAD):
                        left_table()
                        values_rest(1)

                tab = [0]

                def table(ins):
                    tab[0] += 1
                    ins.then_inc(table_step, 1)
                    dve.wait_ge(table_step, tab[0])

                in_bank = bank[7][:, 128:128 + E]

                def experts_of(at, many):
                    table(v.tensor_tensor_scan(tile_end[:, :], ones[:, 0:E], n_tiles[:, :], 0.0, ALU.mult, ALU.add))
                    table(v.tensor_tensor(passed[:, 0:many, :], tile_no[:, 0:many, :],
                                          tile_end[:, :].unsqueeze(1).to_broadcast([P, many, E]), ALU.is_ge))
                    table(v.tensor_reduce(tile_e[:, at], passed[:, 0:many, :], AX_X, ALU.add))
                    table(v.tensor_scalar(w_off[:, at], tile_e[:, at], float(E - 1), float(F), ALU.min, ALU.mult))
                    table(v.tensor_scalar(s_off[:, at], tile_e[:, at], float(E - 1), float(P), ALU.min, ALU.mult))
                    table(v.tensor_tensor(jumps[:, 0:many, :], passed[:, 0:many, :],
                                          jump[:, :].unsqueeze(1).to_broadcast([P, many, E]), ALU.mult))
                    table(v.tensor_reduce(tile_row[:, at], jumps[:, 0:many, :], AX_X, ALU.add))

                most = EARLY_G * G

                def early_counts():
                    dve.wait_ge(counts_psum, 1)
                    v.tensor_tensor(over[:, :, 0:most], in_bank.unsqueeze(2).to_broadcast([P, E, most]),
                                    tile_edges[:, :, 1:most + 1], ALU.is_ge).then_inc(counts_read, 1)

                def early_table():
                    at = slice(0, EARLY)
                    dve.wait_ge(counts_read, 1)
                    table(v.tensor_reduce(n_tiles[:, :], over[:, :, 0:most], AX_X, ALU.add))
                    table(v.tensor_scalar(jump[:, :], n_tiles[:, :], -float(P), float(REGION), ALU.mult, ALU.add))
                    experts_of(at, EARLY)
                    v.scalar_tensor_tensor(row_off[:, at], tile_no[:, at, 0], float(P), tile_row[:, at],
                                           ALU.mult, ALU.add).then_inc(early_ready, 1)

                def left_table():
                    table(v.tensor_scalar(early_end[:, 1:], tile_end[:, :], float(EARLY), None, ALU.min))
                    table(v.tensor_tensor(early[:, 0:E], early_end[:, 1:], early_end[:, 0:E], ALU.subtract))
                    table(v.scalar_tensor_tensor(edges_left[:, :, :], early[:, 0:E].unsqueeze(2).to_broadcast([P, E, NT]),
                                                 float(P), tile_edges[:, :, :], ALU.mult, ALU.add))
                    table(v.tensor_tensor(jump_left[:, :], early[:, 1:], early[:, 0:E], ALU.subtract))
                    table(v.tensor_scalar(jump_left[:, :], jump_left[:, :], float(P), float(REGION), ALU.mult, ALU.add))
                    table(v.tensor_scalar(left_no[:, :], tile_no[:, 0:LEFT, 0], early[:, 0:1], None, ALU.add))

                def late_table():
                    at = slice(EARLY, TILES)
                    dve.wait_ge(counts_psum, 2)
                    v.tensor_tensor(pad_off[:, :], in_bank, region0[:, 0, :], ALU.add).then_inc(pads_known, 1)
                    table(v.tensor_tensor(over[:, :, :], in_bank.unsqueeze(2).to_broadcast([P, E, NT]),
                                          edges_left[:, :, :], ALU.is_gt))
                    table(v.tensor_reduce(n_tiles[:, :], over[:, :, :], AX_X, ALU.add))
                    table(v.scalar_tensor_tensor(jump[:, :], n_tiles[:, :], -float(P), jump_left[:, :], ALU.mult, ALU.add))
                    experts_of(at, LEFT)
                    v.scalar_tensor_tensor(row_off[:, at], left_no[:, :], float(P), tile_row[:, at],
                                           ALU.mult, ALU.add).then_inc(table_ready, 1)

                def values_rest(part):
                    half = slice(part * HALF, part * HALF + HALF)
                    dve.wait_ge(v_hi_ready, G * (NG - 2))
                    v.tensor_tensor(v_lo[:, half], v_sb[:, half], v_hi[:, half], ALU.subtract).then_inc(v_lo_ready, 1)

                def ffn(i, k):
                    if a := ffn_tile(i, k, 2):
                        t, c, _ = a
                        dve.wait_ge(xsT_ready, t + 1)
                        if second_on(t):
                            dve.wait_ge(val_psum, t - 1)
                        v.tensor_tensor(xsT_lo[:, c % 2, :], bank[0][:, 0:P], xsT_hi[:, c % 2, :],
                                        ALU.subtract).then_inc(xsT_lo_ready, 1)
                    if a := ffn_tile(i, k, 1):
                        t, c, _ = a
                        dve.wait_ge(val_psum, t + 1)
                        dve.wait_ge(act_ready, t + 1)
                        if second_on(t):
                            dve.wait_ge(hidT_psum, t - 1)
                        v.tensor_tensor(hid[:, c % 2, :], bank[3 + c % 2][:, :], act_sb[:, c % 2, :],
                                        ALU.mult).then_inc(hid_ready, 1)
                    if a := ffn_tile(i, k, -1):
                        t, c, r = a
                        if isinstance(t, int) and t == 0:
                            dve.wait_ge(ld_s1, 16)
                        off = dve.value_load(s_off[0:1, bass.ds(t, 1)], min_val=0, max_val=(E - 1) * P)
                        dve.wait_ge(y_psum, t + 1)
                        v.scalar_tensor_tensor(yo[:, c % XB, :], bank[6][:, 0:P], xs[:, c % XB, P + 1:P + 2],
                                               s1_sb[:, bass.ds(off, P)], ALU.mult, ALU.mult).then_inc(yo_ready, 1)
                attention_steps(dve, step)
                last_steps(step, ffn, late_table)
                ffn_steps(dve, ffn)

                for g in range(NG):
                    dve.wait_ge(got_rows[g], 16)
                    two = got[g].rearrange("p (t k d) -> p t k d", t=G, k=TOP)
                    part = fin[:, g, 0:G * P].rearrange("p (t d) -> p t d", t=G)
                    v.tensor_tensor(part, two[:, :, 0, :], two[:, :, 1, :], ALU.add).then_inc(pair_sum, 1)
                    dve.wait_ge(pair_sum, g + 1)
                    at = x_sb[:, G * g:G * g + G, :]
                    v.tensor_tensor(at, at, part, ALU.add).then_inc(fin_ready, 1)


_INS = ['x', 'ctx_1024', 'L0_xattn_Wq', 'L0_xattn_bq', 'L0_xattn_Wk', 'L0_xattn_bk', 'L0_xattn_Wv', 'L0_xattn_bv',
        'L0_xattn_Wo', 'L0_xattn_bo', 'L0_ffn_router_w', 'L0_ffn_wv', 'L0_ffn_sv', 'L0_ffn_w', 'L0_ffn_s',
        'L0_ffn_w1', 'L0_ffn_s1']
_OUTS = [((16, 128, 128), 'float32')]


def kernel(**inputs):
    import numpy as _np
    import concourse.bacc as _bacc
    from concourse import mybir as _mybir
    from concourse.bass_utils import run_bass_kernel_spmd as _run

    nc = _bacc.Bacc("TRN2", target_bir_lowering=False, num_devices=1)
    arrays, args = {}, []
    for name in _INS:
        a = _np.ascontiguousarray(inputs[name])
        arrays[f"in_{name}_dram"] = a
        args.append(nc.dram_tensor(f"in_{name}_dram", a.shape, _mybir.dt.from_np(a.dtype), kind="ExternalInput").ap())
    for i, (shape, dtype) in enumerate(_OUTS):
        dt = _mybir.dt.from_np(_np.dtype(dtype))
        args.append(nc.dram_tensor(f"out_{i}_dram", shape, dt, kind="ExternalOutput").ap())
    xattn_moe_kernel(nc, *args)
    r = _run(nc, [arrays], core_ids=[0])
    got = tuple(r.results[0][f"out_{i}_dram"] for i in range(len(_OUTS)))
    return got[0]
```

```python
from contextlib import ExitStack

import concourse.bass as bass
from concourse import mybir

ALU = mybir.AluOpType
ACT = mybir.ActivationFunctionType
AX_X = mybir.AxisListType.X
F32 = mybir.dt.float32
I32 = mybir.dt.int32
U32 = mybir.dt.uint32

P = 128
NT = 16
G = 4
NG = NT // G
H = 16
HD = 8
DK = 64
QW = (HD + 1) * H
E = 8
F = 512
FC = F // P
TOP = 2
ROWW = P + 2
TOKENS = NT * P
REGION = TOKENS + P
TILES = (TOP * TOKENS + E * (P - 1)) // P
SPARE = TOP * G
assert SPARE >= TILES - TOP * TOKENS // P
EARLY_G = NG // 2
EARLY = -(-(TOP * TOKENS * EARLY_G // NG - E * (P - 1)) // P)
LEFT = TILES - EARLY
ROWS = E * REGION + SPARE * P
NOWHERE = 1 << 20
XB = 12
EPS = 1e-5
SCALE = DK ** -0.5


def xattn_moe_kernel(nc, x, ctx, Wq, bq, Wk, bk, Wv, bv, Wo, bo, router_w, wv, sv, w, s, w1, s1, out):
    stack = ExitStack()
    with stack:
        def sb(name, shape, dt=F32):
            return stack.enter_context(nc.sbuf_tensor(name, shape, dt))

        def sem(name):
            return stack.enter_context(nc.semaphore(name))

        bank = [stack.enter_context(nc.psum_tensor(f"bank{i}", [P, 512], F32)) for i in range(8)]

        routed = nc.dram_tensor("routed", [ROWS, ROWW], F32, kind="Internal").ap()
        expert_out = nc.dram_tensor("expert_out", [TOP * TOKENS, P], F32, kind="Internal").ap()

        ident = sb("ident", [P, P])
        ones = sb("ones", [P, P])
        before = sb("before", [P, P])
        head_mask = sb("head_mask", [P, H])
        minus_half = sb("minus_half", [P, NT])
        eps = sb("eps", [P, NT])
        pause_dve, pause_act = sb("pause_dve", [P, 2]), sb("pause_act", [P, 1])
        expert_no = sb("expert_no", [P, G, E])
        region0 = sb("region0", [P, G, E])
        tile_edges = sb("tile_edges", [P, E, NT])
        tile_no = sb("tile_no", [P, TILES, E])
        pad_rows = sb("pad_rows", [P, ROWW])

        q9 = sb("q9", [HD + 1, DK])
        k9 = sb("k9", [HD + 1, DK])
        v9 = sb("v9", [HD + 1, 2 * DK])
        qT = sb("qT", [DK, HD + 1])
        kT = sb("kT", [DK, HD + 1])
        vT = sb("vT", [P, HD + 1])
        qT_rep = sb("qT_rep", [DK, H, HD])
        bq_rep = sb("bq_rep", [DK, P])
        wv2 = sb("wv2", [P, 2 * HD + 1])
        wo_sb = sb("wo_sb", [P, HD, P])
        out_bias = sb("out_bias", [HD + 1, P])
        o_projT = sb("o_projT", [P, P])
        out_biasT = sb("out_biasT", [P, HD])
        q_proj = sb("q_proj", [P, HD + 1, H])
        q_bias = sb("q_bias", [P, HD + 1, H])
        o_proj = sb("o_proj", [P, P])
        router = sb("router", [P, E])

        x_sb = sb("x_sb", [P, NT, P])
        ctx_sb = sb("ctx_sb", [P, NT, P])
        ctx_ig = sb("ctx_ig", [P, NT, HD, H])
        stats = sb("stats", [P, NT, 6])
        mv = sb("mv", [P, NT, 2])
        rstd = sb("rstd", [P, NT])
        shift = sb("shift", [P, NT])
        vtmp = sb("vtmp", [P, NT])

        xn = sb("xn", [P, 2, P])
        xnT = sb("xnT", [P, 2, P])
        q_sb = sb("q_sb", [P, 2, HD + 1, H])
        qk = sb("qk", [P, 2, HD, H * H])
        neg_max = sb("neg_max", [P, 2, H])
        shifted = sb("shifted", [P, 2, H, H])
        sums_in = sb("sums_in", [P, 2, P + H, H])
        rowinv = sb("rowinv", [P, 2, H])
        pv, probs = sums_in[:, :, 0:P, :], sums_in[:, :, P:P + H, :]
        z0 = sb("z0", [P, 2, P + H])
        z = sb("z", [P, 2, P])
        zT = sb("zT", [P, 2, P])

        stats2 = sb("stats2", [P, G, 6])
        mv2 = sb("mv2", [P, G, 2])
        vtmp2 = sb("vtmp2", [P, G])
        rstd2 = sb("rstd2", [P, G])
        shift2 = sb("shift2", [P, G])
        rows_of = [sb(f"rows{b}", [P, G, TOP, ROWW]) for b in range(2)]
        dest = sb("dest", [P, NT, TOP])
        gates_of = [sb(f"gates{b}", [P, G, TOP]) for b in range(2)]
        xn2 = sb("xn2", [P, G, P])
        xn2T = sb("xn2T", [P, G, P])
        top8 = sb("top8", [P, G, E])
        order = sb("order", [P, G, E], U32)
        r2 = sb("r2", [P, G, E + TOP])
        r3 = sb("r3", [P, G, E + TOP])
        r_sum = sb("r_sum", [P, G])
        r_inv = sb("r_inv", [P, G])
        pick = sb("pick", [P, TOP, G, E])
        picked = sb("picked", [P, G, E])
        group_sum = sb("group_sum", [P, E])
        carry = sb("carry", [P, E])
        slot = sb("slot", [P, G, E])
        slot_of = sb("slot_of", [P, TOP, G, E])
        place = sb("place", [P, TOP, G])
        pos_of = [sb(f"pos{b}", [P, TOP, G], I32) for b in range(2)]

        over = sb("over", [P, E, NT])
        n_tiles = sb("n_tiles", [P, E])
        tile_end = sb("tile_end", [P, E])
        jump = sb("jump", [P, E])
        passed = sb("passed", [P, TILES, E])
        jumps = sb("jumps", [P, TILES, E])
        tile_e = sb("tile_e", [P, TILES])
        tile_row = sb("tile_row", [P, TILES])
        w_off = sb("w_off", [P, TILES], I32)
        s_off = sb("s_off", [P, TILES], I32)
        row_off = sb("row_off", [P, TILES], I32)
        pad_off = sb("pad_off", [P, E], I32)

        early_end = sb("early_end", [P, 1 + E])
        early = sb("early", [P, E + 1])
        edges_left = sb("edges_left", [P, E, NT])
        jump_left = sb("jump_left", [P, E])
        left_no = sb("left_no", [P, LEFT])

        g_sb = sb("g_sb", [P, E * F])
        v_sb = sb("v_sb", [P, E * F])
        g_scale = sb("g_scale", [P, E * F])
        w1_sb = sb("w1_sb", [P, E * F])
        xs = sb("xs", [P, XB, ROWW])
        xsT = sb("xsT", [P, 2, P])
        g_tile = sb("g_tile", [P, 2, F])
        v_tile = sb("v_tile", [P, 2, F])
        yo = sb("yo", [P, XB, P])
        sv_rows = sb("sv_rows", [E * FC, P])
        sv_col = sb("sv_col", [P, E * FC])
        s1_sb = wo_sb[:, :, :].rearrange("p c n -> p (c n)")
        ctx_flat = ctx_sb[:, :, :].rearrange("p t n -> p (t n)")
        act_sb = ctx_flat[:, 0:2 * F].rearrange("p (b n) -> p b n", b=2)
        hid = ctx_flat[:, 2 * F:4 * F].rearrange("p (b n) -> p b n", b=2)
        xs_i = xs[:, :, :].bitcast(I32)
        got = [sums_in[:, g // 2, (g % 2) * (P // 2):(g % 2 + 1) * (P // 2), :].rearrange("p m g -> p (m g)")
               for g in range(NG)]
        fin = qk[:, :, :, :].rearrange("p a (q i) s -> p (a q) (i s)", q=2)

        ld_small, ld_wo, ld_bo, ld_router, ld_sv = (sem(n) for n in (
            "ld_small", "ld_wo", "ld_bo", "ld_router", "ld_sv"))
        ld_x = [sem(f"ld_x{g}") for g in range(NG)]
        ld_ctx = [sem(f"ld_ctx{g}") for g in range(NG)]
        ld_wv, ld_wg, ld_gs, ld_w1, ld_s1 = (sem(n) for n in ("ld_wv", "ld_wg", "ld_gs", "ld_w1", "ld_s1"))
        pool_set = sem("pool_set")
        setup_pe, setup_dve, setup_step = sem("setup_pe"), sem("setup_dve"), sem("setup_step")
        ln1_mv, ln1_rstd, ln1_shift = sem("ln1_mv"), sem("ln1_rstd"), sem("ln1_shift")
        ln1_eps = sem("ln1_eps")
        ln1_stats = sem("ln1_stats")
        ctx_turned = sem("ctx_turned")
        xn_ready, xnT_psum, xnT_ready = sem("xn_ready"), sem("xnT_psum"), sem("xnT_ready")
        q_psum, q_ready, qk_ready = sem("q_psum"), sem("q_ready"), sem("qk_ready")
        s_psum, max_ready, s_shifted = sem("s_psum"), sem("max_ready"), sem("s_shifted")
        p_ready, inv_ready = sem("p_ready"), sem("inv_ready")
        pv_ready, z0_ready, z_ready = (sem(n) for n in ("pv_ready", "z0_ready", "z_ready"))
        zT_psum, zT_ready, o_psum, x2_ready = (sem(n) for n in ("zT_psum", "zT_ready", "o_psum", "x2_ready"))
        sv_ready = sem("sv_ready")
        st2_ready, w1_scaled, g_scaled = sem("st2_ready"), sem("w1_scaled"), sem("g_scaled")
        mv2_ready, eps2_ready, rstd2_ready, shift2_ready = (
            sem(n) for n in ("mv2_ready", "eps2_ready", "rstd2_ready", "shift2_ready"))
        xn2_ready, carry_ready, meta_ready = sem("xn2_ready"), sem("carry_ready"), sem("meta_ready")
        rows_ready, xn2T_psum, xn2T_ready, logits_psum = (
            sem(n) for n in ("rows_ready", "xn2T_psum", "xn2T_ready", "logits_psum"))
        logits_shifted, logits_exp, picked_ready, gates_ready, rank_psum, pos_ready = (
            sem(n) for n in ("logits_shifted", "logits_exp", "picked_ready", "gates_ready", "rank_psum", "pos_ready"))
        route_step = sem("route_step")
        scattered = sem("scattered")
        counts_psum, counts_read, table_step, early_ready, pads_known, table_ready, padded = (
            sem(n) for n in ("counts_psum", "counts_read", "table_step", "early_ready", "pads_known", "table_ready", "padded"))
        xs_loaded = [sem(f"xs_loaded{b}") for b in range(XB)]
        y_sent = [sem(f"y_sent{b}") for b in range(XB)]
        xsT_psum, xsT_ready, gate_psum, val_psum = (
            sem(n) for n in ("xsT_psum", "xsT_ready", "gate_psum", "val_psum"))
        g_tile_ready, v_tile_ready = sem("g_tile_ready"), sem("v_tile_ready")
        act_ready, hid_ready, y_psum, yo_ready = (sem(n) for n in ("act_ready", "hid_ready", "y_psum", "yo_ready"))
        CHUNKS = [(0, 4), (4, 4), (8, 4), (12, 3), (15, 1)]
        got_rows = [sem(f"got_rows{n}") for n in range(len(CHUNKS))]
        pair_sum, fin_ready, stored = sem("pair_sum"), sem("fin_ready"), sem("stored")

        POOL_SET, EPS_SET = 16, 7
        SHARE = E * FC // (G * (NG - 2))
        AHEAD = 2
        NORM, LOGITS, PLACES = 7, 8, 9

        def sends(n):
            return {9: 2, 10: 2 if n == EARLY_G - 1 else 3, 11: G * TOP}


        GATES_SCALED = (0, 0, 0, 0, 2, 1, 1, 2, 2)
        assert sum(GATES_SCALED) == E

        def tile_at(g, j, lag):
            t = g * G + (AHEAD + j - lag)
            if isinstance(t, int) and not 0 <= t < NT:
                return None
            return t, (AHEAD + j - lag) % 2

        def group_at(g, j, lag):
            if (AHEAD + j - lag) % G:
                return None
            n = g + (AHEAD + j - lag) // G
            return None if isinstance(n, int) and not 0 <= n < NG else (n,)

        def last_group(n):
            return isinstance(n, int) and n == NG - 1

        def second_on(t):
            return not isinstance(t, int) or t >= 2

        def first_on(t):
            return not isinstance(t, int) or t >= 1

        def attention_steps(eng, step):
            for g in (-1, 0):
                for j in range(G):
                    step(g, j)
            with eng.Fori(1, NG - 1) as g:
                for j in range(G):
                    step(g, j)
            for j in range(AHEAD):
                step(NG - 1, j)

        def got_of(t0, many):
            return got[t0 // G][:, t0 % G * TOP * P:(t0 % G + many) * TOP * P].rearrange("p (t n) -> p t n", t=many)

        def values(eng, t, b):
            return eng.tensor_tensor(pv[:, b, :, :].rearrange("p (h i) g -> p h i g", h=H),
                                     probs[:, b, :, :].unsqueeze(2).to_broadcast([P, H, HD, H]),
                                     ctx_ig[:, t, :, :].unsqueeze(1).to_broadcast([P, H, HD, H]), ALU.mult)

        SENT = 16 * G * TOP
        full = (TILES - 3) // XB
        assert TILES - 3 == full * XB

        EARLY_STEPS = 4

        def ffn_steps(eng, ffn):
            for k in range(EARLY_STEPS, XB):
                ffn(0, k)
            with eng.Fori(1, full) as i:
                for k in range(XB):
                    ffn(i, k)
            for k in range(2):
                ffn(full, k)

        def ffn_tile(i, k, ahead, stages):
            if ahead not in stages:
                return None
            c = 1 + k + ahead
            if isinstance(i, int) and not 0 <= i * XB + c < TILES:
                return None
            return i * XB + c, c, i

        def uses(i, c):
            return i + (c // XB + 1)

        twice = lambda w: w.unsqueeze(1).to_broadcast([w.shape[0], 2, DK])
        SMALL = ((q9[0:HD, :], Wq), (k9[0:HD, :], Wk), (q9[HD:HD + 1, :], bq.unsqueeze(0)),
                 (v9[0:HD, :].rearrange("p (a v) -> p a v", a=2), twice(Wv)), (k9[HD:HD + 1, :], bk.unsqueeze(0)),
                 (v9[HD:HD + 1, :].rearrange("p (a v) -> p a v", a=2), twice(bv.unsqueeze(0))))

        with nc.Block() as block:

            @block.sync
            def _(sp):
                at = [slice(g * G, g * G + G) for g in range(NG)]
                x_t, ctx_t = x.rearrange("t p d -> p t d"), ctx.rearrange("t p d -> p t d")
                sp.dma_start(x_sb[:, at[0], :], x_t[:, at[0], :]).then_inc(ld_x[0], 16)
                for to, frm in SMALL[1::2]:
                    sp.dma_start(to, frm).then_inc(ld_small, 16)
                sp.dma_start(ctx_sb[:, at[0], :], ctx_t[:, at[0], :]).then_inc(ld_ctx[0], 16)
                for g in range(1, NG):
                    sp.dma_start(x_sb[:, at[g], :], x_t[:, at[g], :]).then_inc(ld_x[g], 16)
                for g in range(1, NG):
                    sp.dma_start(ctx_sb[:, at[g], :], ctx_t[:, at[g], :]).then_inc(ld_ctx[g], 16)
                sp.wait_ge(ld_ctx[NG - 1], 16)
                sp.dma_start(g_sb[:, :].rearrange("p (e f) -> p e f", e=E), w.rearrange("e d f -> d e f")).then_inc(ld_wg, 16)
                sp.dma_start(g_scale[:, :], s.rearrange("e a f -> (e a f)").partition_broadcast(P)).then_inc(ld_gs, 16)
                sp.dma_start(w1_sb[:, :].rearrange("p (e c n) -> p e c n", e=E, c=FC),
                             w1.rearrange("e (c p) n -> p e c n", p=P)).then_inc(ld_w1, 16)
                sp.dma_start(v_sb[:, :].rearrange("p (e f) -> p e f", e=E), wv.rearrange("e d f -> d e f")).then_inc(ld_wv, 16)
                sp.wait_ge(setup_pe, 3)
                sp.dma_start(s1_sb[:, :], s1.rearrange("e a n -> (e a n)").partition_broadcast(P)).then_inc(ld_s1, 16)


                def load(i, c):
                    if not (isinstance(i, int) and i == 0):
                        sp.wait_ge(y_sent[c], 16 * i)
                    r0 = sp.value_load(row_off[0:1, bass.ds(i * XB + c, 1)], min_val=0, max_val=ROWS - P)
                    sp.dma_start(xs[:, c, :], routed[bass.ds(r0, P), :]).then_inc(xs_loaded[c], 16)

                sp.wait_ge(early_ready, 1)
                sp.wait_ge(scattered, SENT * (EARLY_G + 1))
                for c in range(EARLY):
                    load(0, c)
                sp.wait_ge(pads_known, 1)
                for e in range(E):
                    r0 = sp.value_load(pad_off[0:1, e:e + 1], min_val=0, max_val=ROWS - P)
                    sp.dma_start(routed[bass.ds(r0, P), :], pad_rows[:, :]).then_inc(padded, 16)
                sp.wait_ge(table_ready, 1)
                sp.wait_ge(padded, 16 * E)
                sp.wait_ge(scattered, SENT * (NG + 1))
                whole = TILES // XB
                for c in range(EARLY, XB):
                    load(0, c)
                with sp.Fori(1, whole) as i:
                    for c in range(XB):
                        load(i, c)
                for c in range(TILES - whole * XB):
                    load(whole, c)

                for b in range(XB):
                    sp.wait_ge(y_sent[b], 16 * len(range(b, TILES, XB)))
                pairs = expert_out.rearrange("(t p k) d -> p t (k d)", p=P, k=TOP)
                out_rows = out.rearrange("t p d -> p t d")
                for n, (t0, many) in enumerate(CHUNKS):
                    sp.dma_start(got_of(t0, many), pairs[:, t0:t0 + many, :]).then_inc(got_rows[n], 16)
                for n, (t0, many) in enumerate(CHUNKS):
                    sp.wait_ge(fin_ready, n + 1)
                    sp.dma_start(out_rows[:, t0:t0 + many, :], x_sb[:, t0:t0 + many, :]).then_inc(stored, 16)
                sp.wait_ge(stored, 16 * len(CHUNKS))

            @block.gpsimd
            def _(pool):
                last_row, last_dest = pool.to_reg(ROWS - 1), pool.to_reg(TOP * TOKENS - 1)
                steps = [0]

                def built(ins):
                    steps[0] += 1
                    ins.then_inc(pool_set, 1)
                    pool.wait_ge(pool_set, steps[0])

                built(pool.memset(ident[:, :], 0.0))
                built(pool.affine_select(out=ident[:, :], in_=ident[:, :], compare_op=ALU.not_equal, fill=1.0,
                                         base=0, pattern=[[-1, P]], channel_multiplier=1))
                built(pool.memset(head_mask[:, :], SCALE))
                built(pool.affine_select(out=head_mask[:, :], in_=head_mask[:, :], compare_op=ALU.is_ge, fill=0.0,
                                         base=0, pattern=[[-HD, H]], channel_multiplier=1))
                built(pool.affine_select(out=head_mask[:, :], in_=head_mask[:, :], compare_op=ALU.is_ge, fill=0.0,
                                         base=HD - 1, pattern=[[HD, H]], channel_multiplier=-1))
                built(pool.memset(minus_half[:, :], -0.5))
                built(pool.memset(eps[:, :], EPS))
                built(pool.memset(ones[:, :], 1.0))
                built(pool.affine_select(out=before[:, :], in_=ones[:, :], compare_op=ALU.is_ge, fill=0.0,
                                         base=-1, pattern=[[1, P]], channel_multiplier=-1))
                built(pool.iota(expert_no[:, :, :], pattern=[[0, G], [1, E]], base=0, channel_multiplier=0,
                                allow_small_or_imprecise_dtypes=True))
                built(pool.iota(region0[:, :, :], pattern=[[0, G], [REGION, E]], base=0, channel_multiplier=0,
                                allow_small_or_imprecise_dtypes=True))
                built(pool.iota(dest[:, :, :], pattern=[[TOP * P, NT], [1, TOP]], base=0, channel_multiplier=TOP,
                                allow_small_or_imprecise_dtypes=True))
                built(pool.iota(tile_edges[:, :, :], pattern=[[0, E], [P, NT]], base=0, channel_multiplier=0,
                                allow_small_or_imprecise_dtypes=True))
                built(pool.iota(tile_no[:, :, :], pattern=[[1, TILES], [0, E]], base=0, channel_multiplier=0,
                                allow_small_or_imprecise_dtypes=True))
                built(pool.memset(pad_rows[:, :], 0.0))
                built(pool.iota(pad_rows[:, P:P + 1].bitcast(I32), pattern=[[0, 1]], base=NOWHERE, channel_multiplier=0))
                assert steps[0] == POOL_SET
                assert 16 * SPARE == SENT and SPARE == 2 * G

                def spare_tile(n):
                    r0 = E * REGION + n * P
                    pool.dma_start(routed[r0:r0 + P, :], pad_rows[:, :]).then_inc(scattered, 16)

                for g in range(NG):
                    if g == 1:
                        for n in range(SPARE):
                            spare_tile(n)
                    at = slice(g * G, g * G + G)
                    pool.wait_ge(ln1_mv, g * G + G)
                    pool.tensor_tensor(vtmp[:, at], mv[:, at, 1], eps[:, at], ALU.add).then_inc(ln1_eps, 1)
                    pool.wait_ge(ln1_eps, g + 1)
                    pool.tensor_tensor(rstd[:, at], vtmp[:, at], minus_half[:, at], ALU.pow).then_inc(ln1_rstd, 1)

                def second_rstd(n):
                    pool.wait_ge(mv2_ready, n * G + G)
                    pool.tensor_tensor(vtmp2[:, :], mv2[:, :, 1], eps[:, 0:G], ALU.add).then_inc(eps2_ready, 1)
                    pool.wait_ge(eps2_ready, n + 1)
                    pool.tensor_tensor(rstd2[:, :], vtmp2[:, :], minus_half[:, 0:G], ALU.pow).then_inc(rstd2_ready, 1)

                def step(g, j):
                    a = tile_at(g, j, 1)
                    if a and a[0] < NT - 1:
                        t, b = a
                        if t in (0, G):
                            pool.wait_ge(ctx_turned, 1 if t == 0 else NG)
                        pool.wait_ge(p_ready, t + 1)
                        if second_on(t):
                            pool.wait_ge(z0_ready, t - 1)
                        values(pool, t, b).then_inc(pv_ready, 1)
                    first, last = (sum(GATES_SCALED[n] for n in range(len(GATES_SCALED)) if n < AHEAD + G * g + j + d) for d in (0, 1))
                    for c in range(first, last):
                        cols = slice(c * F, c * F + F)
                        if c == 0:
                            pool.wait_ge(ld_wg, 16)
                            pool.wait_ge(ld_gs, 16)
                        pool.tensor_tensor(g_sb[:, cols], g_sb[:, cols], g_scale[:, cols], ALU.mult).then_inc(g_scaled, 1)
                    if a := group_at(g, j, NORM - 1):
                        if not last_group(a[0]):
                            second_rstd(a[0])
                    if (g, j) == (NG - 1, G - 1):
                        second_rstd(NG - 1)
                    for lag in sends(0):
                        if a := group_at(g, j, lag):
                            n, = a
                            done = sends(n).get(lag - 1, 0)
                            if done == 0:
                                pool.wait_ge(rows_ready, (n + 2) * TOP)
                                pool.wait_ge(meta_ready, (n + 1) * 2)
                                pool.wait_ge(pos_ready, n + 2)
                            rows, pos = rows_of[last_group(n)], pos_of[last_group(n)]
                            for m in range(done, sends(n)[lag]):
                                pool.indirect_dma_start(
                                    out=routed[:, :],
                                    out_offset=bass.IndirectOffsetOnAxis(ap=pos[:, m % TOP, m // TOP:m // TOP + 1], axis=0),
                                    in_=rows[:, m // TOP, m % TOP, :], in_offset=None,
                                    bounds_check=last_row).then_inc(scattered, 16)

                for t in range(-AHEAD, NT + max(sends(0))):
                    step((t - AHEAD) // G, (t - AHEAD) % G)

                for t in range(TILES):
                    pool.wait_ge(yo_ready, t + 1)
                    pool.indirect_dma_start(
                        out=expert_out[:, :],
                        out_offset=bass.IndirectOffsetOnAxis(ap=xs_i[:, t % XB, P:P + 1], axis=0),
                        in_=yo[:, t % XB, :], in_offset=None,
                        bounds_check=last_dest, oob_is_err=False).then_inc(y_sent[t % XB], 16)

            @block.scalar
            def _(act):
                act.sem_inc(xn2T_ready, 1)
                act.sem_inc(rows_ready, TOP)
                for to, frm in SMALL[0::2]:
                    act.dma_start(to, frm).then_inc(ld_small, 16)
                act.wait_ge(pool_set, EPS_SET)
                nc.scalar.activation(pause_act[:, :], eps[:, 0:1], ACT.Identity)
                act.dma_start(wo_sb[:, :, :], Wo.rearrange("(c p) n -> p c n", p=P)).then_inc(ld_wo, 16)
                act.dma_start(out_bias[HD:HD + 1, :], bo.unsqueeze(0)).then_inc(ld_bo, 16)
                act.dma_start(sv_rows[:, :], sv.rearrange("e a (c p) -> (e a c) p", p=P)).then_inc(ld_sv, 16)
                act.dma_start(router[:, :], router_w).then_inc(ld_router, 16)

                def turn(g):
                    at = slice(g * G, g * G + G)
                    act.wait_ge(ld_ctx[g], 16)
                    nc.scalar.copy(ctx_ig[:, at, :, :],
                                   ctx_sb[:, at, :].rearrange("p t (h i) -> p t i h", h=H)).then_inc(ctx_turned, 1)

                def load_gelu():
                    nc.scalar.activation(pause_act[:, :], eps[:, 0:1], ACT.Gelu_apprx_tanh)

                def step(g, j):
                    if a := tile_at(g, j, -2):
                        t, b = a
                        if isinstance(t, int) and t % G == 0:
                            act.wait_ge(ln1_shift, t // G + 1)
                        if second_on(t):
                            act.wait_ge(xnT_psum, t - 1)
                        nc.scalar.activation(xn[:, b, :], x_sb[:, t, :], ACT.Identity, scale=rstd[:, bass.ds(t, 1)],
                                             bias=shift[:, bass.ds(t, 1)]).then_inc(xn_ready, 1)
                    if a := tile_at(g, j, -1):
                        t, b = a
                        act.wait_ge(q_psum, t + 1)
                        if second_on(t):
                            act.wait_ge(s_psum, t - 1)
                        nc.scalar.copy(q_sb[:, b, :, :].rearrange("p i h -> p (i h)"), bank[1][:, 0:QW]).then_inc(q_ready, 1)
                    if a := tile_at(g, j, 1):
                        t, b = a
                        act.wait_ge(s_shifted, t + 1)
                        if second_on(t):
                            act.wait_ge(z0_ready, t - 1)
                        nc.scalar.activation(probs[:, b, :, :], shifted[:, b, :, :], ACT.Exp).then_inc(p_ready, 1)
                    for n, turns in enumerate(((-1, 0), (-1, 3), (0, 0), (0, 1))):
                        if isinstance(g, int) and (g, j) == turns:
                            turn(n)
                    if a := group_at(g, j, NORM):
                        n, = a
                        act.wait_ge(shift2_ready, n + 1)
                        act.wait_ge(rows_ready, (n + 1) * TOP)
                        act.wait_ge(xn2T_psum, n + 1)
                        for m in range(G):
                            t = n * G + m
                            nc.scalar.activation(xn2[:, m, :], x_sb[:, t, :], ACT.Identity, scale=rstd2[:, m:m + 1],
                                                 bias=shift2[:, m:m + 1]).then_inc(xn2_ready, 1)
                    if isinstance(g, int) and group_at(g, j, LOGITS) == (NG - 2,):
                        turned(NG - 2)
                    if (a := group_at(g, j, LOGITS)) and not isinstance(g, int):
                        logits_exponentials(a[0])
                    if not isinstance(g, int):
                        share = (g - 1) * (G * SHARE) + j * SHARE
                        for c in range(SHARE):
                            chunk = w1_sb[:, bass.ds((share + c) * P, P)]
                            nc.scalar.activation(chunk, chunk, ACT.Copy, scale=sv_col[:, bass.ds(share + c, 1)]).then_inc(w1_scaled, 1)
                    elif (g, j) == (0, G - 1):
                        act.wait_ge(ld_w1, 16)
                        act.wait_ge(sv_ready, 1)
                    if a := tile_at(g, j, -2):
                        t, b = a
                        act.wait_ge(xnT_psum, t + 1)
                        if second_on(t):
                            act.wait_ge(q_psum, t - 1)
                        nc.scalar.copy(xnT[:, b, :], bank[0][:, 0:P]).then_inc(xnT_ready, 1)
                    if (a := group_at(g, j, PLACES)) and not last_group(a[0]):
                        rows_but_gates(a[0])
                    if a := tile_at(g, j, 2):
                        t, b = a
                        act.wait_ge(zT_psum, t + 1)
                        if second_on(t):
                            act.wait_ge(o_psum, t - 1)
                        nc.scalar.copy(zT[:, b, :], bank[4][:, 0:P]).then_inc(zT_ready, 1)
                    if a := tile_at(g, j, 2):
                        t, b = a
                        act.wait_ge(o_psum, t + 1)
                        nc.scalar.copy(x_sb[:, t, :], bank[5][:, 0:P]).then_inc(x2_ready, 1)
                    if (a := group_at(g, j, NORM)) and not (isinstance(g, int) and a == (NG - 2,)):
                        turned(a[0])
                    if a := group_at(g, j, PLACES):
                        n, = a
                        rows, gates = rows_of[last_group(n)], gates_of[last_group(n)]
                        act.wait_ge(gates_ready, n + 1)
                        nc.scalar.copy(rows[:, :, :, P + 1], gates[:, :, :]).then_inc(meta_ready, 1)
                    if (a := group_at(g, j, LOGITS)) and isinstance(g, int):
                        if last_group(a[0]):
                            rows_but_gates(NG - 1)
                        logits_exponentials(a[0])
                        load_gelu()

                def turned(n):
                    act.wait_ge(xn2T_psum, n + 2)
                    act.wait_ge(logits_psum, n + 1)
                    nc.scalar.copy(xn2T[:, :, :].rearrange("p t n -> p (t n)"), bank[6][:, :]).then_inc(xn2T_ready, 1)

                def rows_but_gates(n):
                    act.wait_ge(xn2_ready, n * G + G)
                    rows = rows_of[last_group(n)]
                    rows_i = rows[:, :, :, :].bitcast(I32)
                    if not last_group(n):
                        act.wait_ge(scattered, (n + 1) * SENT)
                    for k in range(TOP):
                        nc.scalar.copy(rows[:, :, k, 0:P], xn2[:, :, :]).then_inc(rows_ready, 1)
                    nc.scalar.copy(rows_i[:, :, :, P], dest[:, bass.ds(n * G, G), :]).then_inc(meta_ready, 1)

                def logits_exponentials(n):
                    act.wait_ge(logits_shifted, n + 1)
                    nc.scalar.activation(r3[:, :, :], r2[:, :, :], ACT.Exp).then_inc(logits_exp, 1)

                def ffn(i, k, stages=(2, 1, 0)):
                    if a := ffn_tile(i, k, 2, stages):
                        t, c, _ = a
                        if isinstance(t, int) and t == 0:
                            act.wait_ge(early_ready, 1)
                            act.wait_ge(g_scaled, E)
                        if isinstance(t, int) and t == EARLY:
                            act.wait_ge(table_ready, 1)
                        at = act.value_load(w_off[0:1, bass.ds(t, 1)], min_val=0, max_val=(E - 1) * F)
                        if second_on(t):
                            act.wait_ge(val_psum, t - 1)
                        nc.scalar.copy(g_tile[:, c % 2, :], g_sb[:, bass.ds(at, F)]).then_inc(g_tile_ready, 1)
                        act.wait_ge(xsT_psum, t + 1)
                        nc.scalar.copy(xsT[:, c % 2, :], bank[0][:, 0:P]).then_inc(xsT_ready, 1)
                    if a := ffn_tile(i, k, 1, stages):
                        t, c, _ = a
                        act.wait_ge(gate_psum, t + 1)
                        if second_on(t):
                            act.wait_ge(hid_ready, t - 1)
                        nc.scalar.activation(act_sb[:, c % 2, :], bank[1 + c % 2][:, :],
                                             ACT.Gelu_apprx_tanh).then_inc(act_ready, 1)

                attention_steps(act, step)
                step(NG - 1, 2)
                ffn(0, -3)
                step(NG - 1, 3)
                ffn(0, -2)
                step(NG, 1)
                ffn(0, -1)
                step(NG, 2)
                ffn(0, 0)
                ffn(0, 1, stages=(2,))
                step(NG, 3)
                ffn(0, 1, stages=(1,))
                ffn(0, 2)
                ffn(0, 3)
                ffn_steps(act, ffn)

            @block.tensor
            def _(pe):
                pe.sem_inc(logits_psum, 1)
                pe.sem_inc(xn2T_psum, 1)
                def keep_warm(many):
                    for _ in range(many):
                        nc.tensor.matmul(bank[7][:, 0:P], ident[:, :], ident[:, :], start=True, stop=True)

                pe.wait_ge(pool_set, 2)
                keep_warm(9)
                pe.wait_ge(ld_small, 16 * len(SMALL))
                nc.tensor.transpose(bank[0][0:DK, 0:HD + 1], q9[:, :], ident[0:HD + 1, 0:HD + 1])
                nc.tensor.transpose(bank[0][0:DK, 16:17 + HD], k9[:, :], ident[0:HD + 1, 0:HD + 1])
                nc.tensor.transpose(bank[0][:, 32:33 + HD], v9[:, :], ident[0:HD + 1, 0:HD + 1]).then_inc(setup_pe, 1)
                keep_warm(6)
                pe.wait_ge(setup_dve, 1)
                nc.tensor.matmul(bank[1][:, 0:HD + 1], qT_rep[:, :, :].rearrange("p h i -> p (h i)"), kT[:, :],
                                 start=True, stop=True)
                nc.tensor.matmul(bank[1][:, 16:17 + HD], bq_rep[:, :], kT[:, :], start=True, stop=True).then_inc(setup_pe, 1)
                keep_warm(4)
                pe.wait_ge(setup_dve, 2)

                def value_product():
                    pe.wait_ge(ld_sv, 16)
                    nc.tensor.transpose(bank[6][:, 0:E * FC], sv_rows[:, :], ident[0:E * FC, 0:E * FC])
                    pe.wait_ge(ld_wo, 16)
                    many = 2 * HD + 1
                    for c in range(HD):
                        mm = nc.tensor.matmul(bank[4][:, c * many:(c + 1) * many], wo_sb[:, c, :], wv2[:, :],
                                              start=True, stop=True)
                    mm.then_inc(setup_pe, 1)

                def value_turned():
                    pe.wait_ge(setup_dve, 5)
                    nc.tensor.transpose(bank[5][:, 0:P], o_projT[:, :], ident[:, :])
                    nc.tensor.transpose(bank[5][0:HD, P:2 * P], out_biasT[:, :], ident[:, :]).then_inc(setup_pe, 1)

                def step(g, j):
                    if a := tile_at(g, j, -1):
                        t, b = a
                        pe.wait_ge(xnT_ready, t + 1)
                        if first_on(t):
                            pe.wait_ge(q_ready, t)
                        else:
                            pe.wait_ge(setup_dve, 4)
                        nc.tensor.matmul(bank[1][:, 0:QW], xnT[:, b, :], q_proj[:, :, :].rearrange("p i h -> p (i h)"),
                                         start=True, stop=False)
                        nc.tensor.matmul(bank[1][:, 0:QW], ident[:, :], q_bias[:, :, :].rearrange("p i h -> p (i h)"),
                                         start=False, stop=True).then_inc(q_psum, 1)
                    if isinstance(g, int) and (g, j) == (-1, AHEAD):
                        value_product()
                    if a := group_at(g, j, LOGITS):
                        n, = a
                        pe.wait_ge(xn2T_ready, n + 2)
                        pe.wait_ge(pos_ready, n + 1)
                        if isinstance(n, int) and n == EARLY_G:
                            pe.wait_ge(counts_read, 1)
                        for m in range(G):
                            mm = nc.tensor.matmul(bank[7][:, m * E:m * E + E], xn2T[:, m, :], router[:, :],
                                                  start=True, stop=True)
                        mm.then_inc(logits_psum, 1)
                    if a := tile_at(g, j, -2):
                        t, b = a
                        pe.wait_ge(xn_ready, t + 1)
                        if first_on(t):
                            pe.wait_ge(xnT_ready, t)
                        nc.tensor.transpose(bank[0][:, 0:P], xn[:, b, :], ident[:, :]).then_inc(xnT_psum, 1)
                        if isinstance(t, int) and t < 2:
                            keep_warm(2)
                    if a := tile_at(g, j, 0):
                        t, b = a
                        pe.wait_ge(qk_ready, t + 1)
                        if second_on(t):
                            pe.wait_ge(s_shifted, t - 1)
                        nc.tensor.matmul(bank[2 + b][:, 0:H * H], ident[:, :],
                                         q_sb[:, b, HD, :].unsqueeze(2).to_broadcast([P, H, H]), start=True, stop=False)
                        for i in range(HD):
                            mm = nc.tensor.matmul(bank[2 + b][:, 0:H * H], ident[:, :], qk[:, b, i, :],
                                                  start=False, stop=(i == HD - 1))
                        mm.then_inc(s_psum, 1)
                    if (a := group_at(g, j, LOGITS)) and not isinstance(g, int):
                        places(a[0])
                    if a := tile_at(g, j, 2):
                        t, b = a
                        if not first_on(t):
                            pe.wait_ge(sv_ready, 1)
                            pe.wait_ge(ld_bo, 16)
                        pe.wait_ge(z_ready, t + 1)
                        if first_on(t):
                            pe.wait_ge(zT_ready, t)
                        nc.tensor.transpose(bank[4][:, 0:P], z[:, b, :], ident[:, :]).then_inc(zT_psum, 1)
                    if a := tile_at(g, j, 2):
                        t, b = a
                        pe.wait_ge(zT_ready, t + 1)
                        if first_on(t):
                            pe.wait_ge(x2_ready, t)
                        nc.tensor.matmul(bank[5][:, 0:P], zT[:, b, :], o_proj[:, :], start=True, stop=False)
                        nc.tensor.matmul(bank[5][:, 0:P], ones[0:HD + 1, :], out_bias[:, :], start=False, stop=False)
                        nc.tensor.matmul(bank[5][:, 0:P], ident[:, :], x_sb[:, t, :], start=False, stop=True).then_inc(o_psum, 1)
                    if a := group_at(g, j, NORM):
                        n, = a
                        pe.wait_ge(xn2T_ready, n + 1)
                        for m in range(G):
                            pe.wait_ge(xn2_ready, n * G + (m + 1))
                            mm = nc.tensor.transpose(bank[6][:, m * P:m * P + P], xn2[:, m, :], ident[:, :])
                        mm.then_inc(xn2T_psum, 1)
                    if isinstance(g, int) and (g, j) == (-1, 3):
                        value_turned()
                    if isinstance(g, int) and (g, j) == (0, G - 1):
                        pe.wait_ge(ld_router, 16)
                    if isinstance(g, int) and (g, j) == (NG - 1, 0):
                        counts(EARLY_G)
                    if isinstance(g, int) and group_at(g, j, LOGITS) == (NG - 2,):
                        places(NG - 2)

                def places(n):
                    pe.wait_ge(picked_ready, n + 1)
                    rank = bank[7][:, 64:64 + G * E]
                    flat = picked[:, :, :].rearrange("p t e -> p (t e)")
                    nc.tensor.matmul(rank, before[:, :], flat, start=True, stop=False)
                    for m in range(1, G):
                        nc.tensor.matmul(rank[:, m * E:], ones[:, :], flat[:, 0:(G - m) * E], start=False, stop=False)
                    nc.tensor.matmul(rank, ones[:, :], carry[:, :].unsqueeze(1).to_broadcast([P, G, E]),
                                     start=False, stop=True).then_inc(rank_psum, 1)

                def counts(groups):
                    pe.wait_ge(carry_ready, groups)
                    nc.tensor.matmul(bank[7][:, 128:128 + E], ones[:, :], carry[:, :], start=True, stop=True).then_inc(counts_psum, 1)

                found = {}

                def weights_of(t):
                    if isinstance(t, int) and t in (0, EARLY):
                        pe.wait_ge(early_ready if t == 0 else table_ready, 1)
                    return pe.value_load(w_off[0:1, bass.ds(t, 1)], min_val=0, max_val=(E - 1) * F)

                def ffn(i, k, stages=(2, 1, 0)):
                    if a := ffn_tile(i, k, 2, stages):
                        t, c, r = a
                        pe.wait_ge(xs_loaded[c % XB], uses(r, c) * 16)
                        if first_on(t):
                            pe.wait_ge(xsT_ready, t)
                        nc.tensor.transpose(bank[0][:, 0:P], xs[:, c % XB, 0:P], ident[:, :]).then_inc(xsT_psum, 1)
                    if a := ffn_tile(i, k, 1, stages):
                        t, c, _ = a
                        pe.wait_ge(g_tile_ready, t + 1)
                        pe.wait_ge(v_tile_ready, t + 1)
                        pe.wait_ge(xsT_ready, t + 1)
                        if second_on(t):
                            pe.wait_ge(hid_ready, t - 1)
                        for psum, weights, ready in ((bank[1 + c % 2], g_tile, gate_psum), (bank[3 + c % 2], v_tile, val_psum)):
                            for n in range(FC):
                                mm = nc.tensor.matmul(psum[:, n * P:n * P + P], weights[:, c % 2, n * P:n * P + P],
                                                      xsT[:, c % 2, :], start=True, stop=True)
                            mm.then_inc(ready, 1)
                        if k + 1 < XB:
                            found[c] = weights_of(t)
                    if a := ffn_tile(i, k, 0, stages):
                        t, c, _ = a
                        y_at = found.pop(c) if c in found else weights_of(t)
                        if isinstance(t, int) and t == 0:
                            pe.wait_ge(w1_scaled, E * FC)
                        pe.wait_ge(hid_ready, t + 1)
                        if second_on(t):
                            pe.wait_ge(yo_ready, t - 1)
                        elif t == 0:
                            pe.wait_ge(x2_ready, NT)
                        else:
                            pe.wait_ge(xn2T_ready, NG + 1)
                        for n in range(FC):
                            mm = nc.tensor.matmul(bank[5 + c % 2][:, 0:P], hid[:, c % 2, n * P:n * P + P],
                                                  w1_sb[:, bass.ds(y_at + n * P, P)], start=(n == 0), stop=(n == FC - 1))
                        mm.then_inc(y_psum, 1)

                attention_steps(pe, step)
                step(NG - 1, 2)
                ffn(0, -3)
                step(NG - 1, 3)
                ffn(0, -2)
                ffn(0, -1, stages=(2,))
                step(NG, 1)
                ffn(0, -1, stages=(1,))
                step(NG, 2)
                ffn(0, -1, stages=(0,))
                ffn(0, 0, stages=(2, 1))
                places(NG - 1)
                ffn(0, 0, stages=(0,))
                ffn(0, 1, stages=(2,))
                counts(NG)
                ffn(0, 1, stages=(1, 0))
                ffn(0, 2, stages=(1,))
                ffn(0, 2, stages=(2, 0))
                ffn(0, 3)
                ffn_steps(pe, ffn)

            @block.vector
            def _(dve):
                v = nc.vector
                chain = [0]

                def small(ins):
                    chain[0] += 1
                    ins.then_inc(setup_step, 1)
                    dve.wait_ge(setup_step, chain[0])

                dve.sem_inc(pos_ready, 1)
                small(v.memset(wv2[:, :], 0.0))
                small(v.memset(carry[:, :], 0.0))
                small(v.memset(early_end[:, 0:1], 0.0))
                small(v.memset(early[:, E:], 0.0))
                def statistics(g):
                    dve.wait_ge(ld_x[g], 16)
                    for t in range(g * G, g * G + G):
                        v.bn_stats(stats[:, t, :], x_sb[:, t, :]).then_inc(ln1_stats, 1)
                    for t in range(g * G, g * G + G):
                        dve.wait_ge(ln1_stats, t + 1)
                        v.bn_aggr(mv[:, t, :], stats[:, t, :]).then_inc(ln1_mv, 1)

                def shifts(g):
                    at = slice(g * G, g * G + G)
                    dve.wait_ge(ln1_rstd, g + 1)
                    dve.wait_ge(ln1_mv, g * G + G)
                    v.scalar_tensor_tensor(shift[:, at], mv[:, at, 0], -1.0, rstd[:, at], ALU.mult, ALU.mult).then_inc(ln1_shift, 1)

                statistics(0)
                dve.wait_ge(setup_pe, 1)
                small(v.tensor_copy(qT_rep[:, :, :], bank[0][0:DK, 0:HD].unsqueeze(1).to_broadcast([DK, H, HD])))
                small(v.tensor_copy(bq_rep[:, :], bank[0][0:DK, HD:HD + 1].to_broadcast([DK, P])))
                v.tensor_copy(kT[:, :], bank[0][0:DK, 16:17 + HD]).then_inc(setup_dve, 1)
                small(v.tensor_copy(wv2[:, 2 * HD:], bank[0][:, 32 + HD:33 + HD]))
                for a in range(2):
                    at = slice(a * DK, a * DK + DK)
                    ins = v.tensor_copy(wv2[at, a * HD:(a + 1) * HD], bank[0][at, 32:32 + HD])
                    if a == 0:
                        small(ins)
                ins.then_inc(setup_dve, 1)

                shifts(0)
                dve.wait_ge(setup_pe, 2)
                dve.wait_ge(pool_set, POOL_SET)
                v.tensor_tensor(q_proj[:, :, :], bank[1][:, 0:HD + 1].unsqueeze(2).to_broadcast([P, HD + 1, H]),
                                head_mask[:, :].unsqueeze(1).to_broadcast([P, HD + 1, H]), ALU.mult).then_inc(setup_dve, 1)
                v.tensor_scalar(q_bias[:, :, :], bank[1][:, 16:17 + HD].unsqueeze(2).to_broadcast([P, HD + 1, H]),
                                SCALE, None, ALU.mult).then_inc(setup_dve, 1)

                for n in range(1, 2):
                    statistics(n)

                def projection_parts():
                    dve.wait_ge(setup_pe, 3)
                    parts = bank[4][:, 0:HD * (2 * HD + 1)].rearrange("p (c n) -> p c n", c=HD)
                    v.tensor_copy(o_projT[:, :].rearrange("p (c n) -> p c n", c=HD), parts[:, :, 0:2 * HD])
                    v.tensor_copy(out_biasT[:, :], parts[:, :, 2 * HD]).then_inc(setup_dve, 1)

                def output_projection():
                    dve.wait_ge(setup_pe, 4)
                    v.tensor_copy(out_bias[0:HD, :], bank[5][0:HD, P:2 * P])
                    v.tensor_copy(o_proj[:, :], bank[5][:, 0:P])
                    v.tensor_copy(sv_col[:, :], bank[6][:, 0:E * FC]).then_inc(sv_ready, 1)

                CHAIN = 13

                def step(g, j):
                    def wide(x):
                        return x.unsqueeze(2).to_broadcast

                    def normalised():
                        out_of, stats_of = tile_at(g, j, 2), tile_at(g, j, 3)
                        m = (AHEAD + j - 3) % G
                        if out_of:
                            t, b = out_of
                            dve.wait_ge(pv_ready, t + 1)
                            v.tensor_reduce(z0[:, b, :], sums_in[:, b, :, :], AX_X, ALU.add).then_inc(z0_ready, 1)
                        if stats_of:
                            t, b = stats_of
                            dve.wait_ge(x2_ready, t + 1)
                            v.bn_stats(stats2[:, m, :], x_sb[:, t, :]).then_inc(st2_ready, 1)
                        if out_of:
                            t, b = out_of
                            dve.wait_ge(z0_ready, t + 1)
                            v.reciprocal(rowinv[:, b, :], z0[:, b, P:P + H]).then_inc(inv_ready, 1)
                        if stats_of:
                            t, b = stats_of
                            dve.wait_ge(st2_ready, t + 1)
                            v.memset(pause_dve[:, 0:1], 0.0)
                            v.bn_aggr(mv2[:, m, :], stats2[:, m, :]).then_inc(mv2_ready, 1)
                        if out_of:
                            t, b = out_of
                            dve.wait_ge(inv_ready, t + 1)
                            if second_on(t):
                                dve.wait_ge(zT_psum, t - 1)
                            v.tensor_tensor(z[:, b, :].rearrange("p (h i) -> p h i", h=H),
                                            z0[:, b, 0:P].rearrange("p (h i) -> p h i", h=H),
                                            rowinv[:, b, :].unsqueeze(2).to_broadcast([P, H, HD]), ALU.mult).then_inc(z_ready, 1)

                    if a := tile_at(g, j, 0):
                        t, b = a
                        if isinstance(t, int) and t in (0, G):
                            dve.wait_ge(ctx_turned, 1 if t == 0 else NG)
                        dve.wait_ge(q_ready, t + 1)
                        if second_on(t):
                            dve.wait_ge(s_psum, t - 1)
                        v.tensor_tensor(qk[:, b, :, :].rearrange("p i (h g) -> p i h g", h=H),
                                        q_sb[:, b, 0:HD, :].unsqueeze(3).to_broadcast([P, HD, H, H]),
                                        ctx_ig[:, t, :, :].unsqueeze(2).to_broadcast([P, HD, H, H]),
                                        ALU.mult).then_inc(qk_ready, 1)
                    if a := tile_at(g, j, 1):
                        t, b = a
                        if isinstance(t, int) and t == 0:
                            projection_parts()
                            for n in range(2, NG):
                                statistics(n)
                        dve.wait_ge(s_psum, t + 1)
                        scores = bank[2 + b][:, 0:H * H].rearrange("p (h g) -> p h g", h=H)
                        v.tensor_reduce(neg_max[:, b, :], scores, AX_X, ALU.max, negate=True).then_inc(max_ready, 1)
                    elif not group_at(g, j, NORM):
                        normalised()
                    if a := tile_at(g, j, 1):
                        t, b = a
                        dve.wait_ge(max_ready, t + 1)
                        if second_on(t):
                            dve.wait_ge(p_ready, t - 1)
                        v.tensor_tensor(shifted[:, b, :, :], scores,
                                        neg_max[:, b, :].unsqueeze(2).to_broadcast([P, H, H]), ALU.add).then_inc(s_shifted, 1)
                        if isinstance(t, int) and t == 0:
                            for n in range(1, NG):
                                shifts(n)
                        if isinstance(t, int) and t == 1:
                            output_projection()
                        if isinstance(t, int) and t == NT - 2:
                            early_counts()
                        if isinstance(t, int) and t == NT - 1:
                            normalised()
                            dve.wait_ge(p_ready, NT)
                            dve.wait_ge(z0_ready, NT - 2)
                            values(v, t, b).then_inc(pv_ready, 1)
                            early_table()
                    if a := group_at(g, j, NORM):
                        n, = a
                        dve.wait_ge(rstd2_ready, n + 1)
                        v.scalar_tensor_tensor(shift2[:, :], mv2[:, :, 0], -1.0, rstd2[:, :],
                                               ALU.mult, ALU.mult).then_inc(shift2_ready, 1)
                        dve.wait_ge(shift2_ready, n + 1)
                    if a := group_at(g, j, LOGITS):
                        n, = a
                        if not isinstance(g, int):
                            normalised()
                        logits = bank[7][:, 0:G * E].rearrange("p (t e) -> p t e", t=G)
                        dve.wait_ge(logits_psum, n + 2)
                        v.memset(pause_dve[:, 1:2], 0.0)
                        for m in range(G):
                            v.max(top8[:, m, :], logits[:, m, :]).then_inc(route_step, 1)
                        dve.wait_ge(route_step, n * CHAIN + 4)
                        v.tensor_tensor(r2[:, :, 0:E], logits, wide(top8[:, :, 0])([P, G, E]), ALU.subtract)
                        v.tensor_tensor(r2[:, :, E:], top8[:, :, 0:TOP], wide(top8[:, :, 0])([P, G, TOP]),
                                        ALU.subtract).then_inc(logits_shifted, 1)
                        for m in range(G):
                            v.max_index(order[:, m, :], top8[:, m, :], logits[:, m, :]).then_inc(route_step, 1)
                        dve.wait_ge(route_step, n * CHAIN + 8)
                        v.tensor_tensor(pick[:, :, :, :], expert_no[:, :, :].unsqueeze(1).to_broadcast([P, TOP, G, E]),
                                        order[:, :, 0:TOP].rearrange("p t k -> p k t").unsqueeze(3).to_broadcast([P, TOP, G, E]),
                                        ALU.is_equal).then_inc(route_step, 1)
                        dve.wait_ge(route_step, n * CHAIN + 9)
                        v.tensor_tensor(picked[:, :, :], pick[:, 0, :, :], pick[:, 1, :, :], ALU.add).then_inc(picked_ready, 1)
                    if a := group_at(g, j, PLACES):
                        n, = a
                        gates, pos = gates_of[last_group(n)], pos_of[last_group(n)]
                        if not last_group(n):
                            dve.wait_ge(scattered, (n + 1) * SENT)
                        dve.wait_ge(logits_exp, n + 1)
                        v.tensor_reduce(r_sum[:, :], r3[:, :, 0:E], AX_X, ALU.add)
                        dve.wait_ge(picked_ready, n + 1)
                        v.tensor_reduce(group_sum[:, :], picked[:, :, :].rearrange("p t e -> p e t"), AX_X, ALU.add)
                        dve.wait_ge(rank_psum, n + 1)
                        rank = bank[7][:, 64:64 + G * E].rearrange("p (t e) -> p t e", t=G)
                        v.tensor_tensor(slot[:, :, :], rank, region0[:, :, :], ALU.add).then_inc(route_step, 1)
                        dve.wait_ge(route_step, n * CHAIN + 10)
                        v.tensor_tensor(slot_of[:, :, :, :], pick[:, :, :, :],
                                        slot[:, :, :].unsqueeze(1).to_broadcast([P, TOP, G, E]), ALU.mult).then_inc(route_step, 1)
                        v.reciprocal(r_inv[:, :], r_sum[:, :]).then_inc(route_step, 1)
                        v.tensor_tensor(carry[:, :], carry[:, :], group_sum[:, :], ALU.add).then_inc(carry_ready, 1)
                        dve.wait_ge(route_step, n * CHAIN + 12)
                        v.tensor_reduce(place[:, :, :], slot_of[:, :, :, :], AX_X, ALU.add).then_inc(route_step, 1)
                        v.tensor_tensor(gates[:, :, :], r3[:, :, E:], wide(r_inv[:, :])([P, G, TOP]), ALU.mult).then_inc(gates_ready, 1)
                        dve.wait_ge(route_step, n * CHAIN + 13)
                        v.tensor_copy(pos[:, :, :], place[:, :, :]).then_inc(pos_ready, 1)
                        dve.wait_ge(carry_ready, n + 1)
                    if (tile_at(g, j, 1) or group_at(g, j, NORM)) and not group_at(g, j, LOGITS):
                        normalised()

                tab = [0]

                def table(ins):
                    tab[0] += 1
                    ins.then_inc(table_step, 1)
                    dve.wait_ge(table_step, tab[0])

                in_bank = bank[7][:, 128:128 + E]

                def experts_of(at, many):
                    table(v.tensor_tensor_scan(tile_end[:, :], ones[:, 0:E], n_tiles[:, :], 0.0, ALU.mult, ALU.add))
                    table(v.tensor_tensor(passed[:, 0:many, :], tile_no[:, 0:many, :],
                                          tile_end[:, :].unsqueeze(1).to_broadcast([P, many, E]), ALU.is_ge))
                    table(v.tensor_reduce(tile_e[:, at], passed[:, 0:many, :], AX_X, ALU.add))
                    table(v.tensor_scalar(w_off[:, at], tile_e[:, at], float(E - 1), float(F), ALU.min, ALU.mult))
                    table(v.tensor_scalar(s_off[:, at], tile_e[:, at], float(E - 1), float(P), ALU.min, ALU.mult))

                def jumps_of(at, many):
                    table(v.tensor_tensor(jumps[:, 0:many, :], passed[:, 0:many, :],
                                          jump[:, :].unsqueeze(1).to_broadcast([P, many, E]), ALU.mult))
                    table(v.tensor_reduce(tile_row[:, at], jumps[:, 0:many, :], AX_X, ALU.add))

                most = EARLY_G * G

                def early_counts():
                    dve.wait_ge(counts_psum, 1)
                    v.tensor_tensor(over[:, :, 0:most], in_bank.unsqueeze(2).to_broadcast([P, E, most]),
                                    tile_edges[:, :, 1:most + 1], ALU.is_ge).then_inc(counts_read, 1)

                def early_table():
                    at = slice(0, EARLY)
                    dve.wait_ge(counts_read, 1)
                    table(v.tensor_reduce(n_tiles[:, :], over[:, :, 0:most], AX_X, ALU.add))
                    table(v.tensor_scalar(jump[:, :], n_tiles[:, :], -float(P), float(REGION), ALU.mult, ALU.add))
                    experts_of(at, EARLY)
                    jumps_of(at, EARLY)
                    v.scalar_tensor_tensor(row_off[:, at], tile_no[:, at, 0], float(P), tile_row[:, at],
                                           ALU.mult, ALU.add).then_inc(early_ready, 1)

                def left_table():
                    table(v.tensor_scalar(early_end[:, 1:], tile_end[:, :], float(EARLY), None, ALU.min))
                    table(v.tensor_tensor(early[:, 0:E], early_end[:, 1:], early_end[:, 0:E], ALU.subtract))
                    table(v.scalar_tensor_tensor(edges_left[:, :, :], early[:, 0:E].unsqueeze(2).to_broadcast([P, E, NT]),
                                                 float(P), tile_edges[:, :, :], ALU.mult, ALU.add))
                    table(v.tensor_tensor(jump_left[:, :], early[:, 1:], early[:, 0:E], ALU.subtract))
                    table(v.tensor_scalar(jump_left[:, :], jump_left[:, :], float(P), float(REGION), ALU.mult, ALU.add))
                    table(v.tensor_scalar(left_no[:, :], tile_no[:, 0:LEFT, 0], early[:, 0:1], None, ALU.add))

                def pads():
                    dve.wait_ge(counts_psum, 2)
                    v.tensor_tensor(pad_off[:, :], in_bank, region0[:, 0, :], ALU.add).then_inc(pads_known, 1)

                late = slice(EARLY, TILES)

                def late_tiles():
                    table(v.tensor_tensor(over[:, :, :], in_bank.unsqueeze(2).to_broadcast([P, E, NT]),
                                          edges_left[:, :, :], ALU.is_gt))
                    table(v.tensor_reduce(n_tiles[:, :], over[:, :, :], AX_X, ALU.add))
                    table(v.scalar_tensor_tensor(jump[:, :], n_tiles[:, :], -float(P), jump_left[:, :], ALU.mult, ALU.add))

                def late_rows():
                    jumps_of(late, LEFT)
                    v.scalar_tensor_tensor(row_off[:, late], left_no[:, :], float(P), tile_row[:, late],
                                           ALU.mult, ALU.add).then_inc(table_ready, 1)

                def ffn(i, k, stages=(2, 1, 0)):
                    if a := ffn_tile(i, k, 2, stages):
                        t, c, _ = a
                        if isinstance(t, int) and t == 0:
                            dve.wait_ge(ld_wv, 16)
                        at = dve.value_load(w_off[0:1, bass.ds(t, 1)], min_val=0, max_val=(E - 1) * F)
                        if second_on(t):
                            dve.wait_ge(val_psum, t - 1)
                        v.tensor_copy(v_tile[:, c % 2, :], v_sb[:, bass.ds(at, F)]).then_inc(v_tile_ready, 1)
                    if a := ffn_tile(i, k, 1, stages):
                        t, c, _ = a
                        dve.wait_ge(val_psum, t + 1)
                        dve.wait_ge(act_ready, t + 1)
                        if second_on(t):
                            dve.wait_ge(y_psum, t - 1)
                        v.tensor_tensor(hid[:, c % 2, :], bank[3 + c % 2][:, :], act_sb[:, c % 2, :],
                                        ALU.mult).then_inc(hid_ready, 1)
                    if a := ffn_tile(i, k, 0, stages):
                        t, c, _ = a
                        if isinstance(t, int) and t == 0:
                            dve.wait_ge(ld_s1, 16)
                        off = dve.value_load(s_off[0:1, bass.ds(t, 1)], min_val=0, max_val=(E - 1) * P)
                        dve.wait_ge(y_psum, t + 1)
                        v.scalar_tensor_tensor(yo[:, c % XB, :], bank[5 + c % 2][:, 0:P], xs[:, c % XB, P + 1:P + 2],
                                               s1_sb[:, bass.ds(off, P)], ALU.mult, ALU.mult).then_inc(yo_ready, 1)

                attention_steps(dve, step)
                step(NG - 1, 2)
                step(NG - 1, 3)
                ffn(0, -3)
                step(NG, 0)
                step(NG, 1)
                ffn(0, -2, stages=(2,))
                left_table()
                ffn(0, -2, stages=(1,))
                ffn(0, -1, stages=(2, 1))
                step(NG, 2)
                ffn(0, 0, stages=(2,))
                ffn(0, -1, stages=(0,))
                step(NG, 3)
                pads()
                ffn(0, 0, stages=(1, 0))
                ffn(0, 1, stages=(2, 1))
                ffn(0, 2, stages=(2,))
                late_tiles()
                ffn(0, 1, stages=(0,))
                ffn(0, 2, stages=(0,))
                ffn(0, 2, stages=(1,))
                ffn(0, 3, stages=(2,))
                experts_of(late, LEFT)
                ffn(0, 3, stages=(1, 0))
                late_rows()
                ffn_steps(dve, ffn)

                for n, (t0, many) in enumerate(CHUNKS):
                    dve.wait_ge(got_rows[n], 16)
                    two = got_of(t0, many).rearrange("p t (k d) -> p t k d", k=TOP)
                    first = t0 % G * P
                    part = fin[:, t0 // G, first:first + many * P].rearrange("p (t d) -> p t d", t=many)
                    v.tensor_tensor(part, two[:, :, 0, :], two[:, :, 1, :], ALU.add).then_inc(pair_sum, 1)
                    dve.wait_ge(pair_sum, n + 1)
                    at = x_sb[:, t0:t0 + many, :]
                    v.tensor_tensor(at, at, part, ALU.add).then_inc(fin_ready, 1)


_INS = ['x', 'ctx_1024', 'L0_xattn_Wq', 'L0_xattn_bq', 'L0_xattn_Wk', 'L0_xattn_bk', 'L0_xattn_Wv', 'L0_xattn_bv',
        'L0_xattn_Wo', 'L0_xattn_bo', 'L0_ffn_router_w', 'L0_ffn_wv', 'L0_ffn_sv', 'L0_ffn_w', 'L0_ffn_s',
        'L0_ffn_w1', 'L0_ffn_s1']
_OUTS = [((16, 128, 128), 'float32')]


def kernel(**inputs):
    import numpy as _np
    import concourse.bacc as _bacc
    from concourse import mybir as _mybir
    from concourse.bass_utils import run_bass_kernel_spmd as _run

    nc = _bacc.Bacc("TRN2", target_bir_lowering=False, num_devices=1)
    arrays, args = {}, []
    for name in _INS:
        a = _np.ascontiguousarray(inputs[name])
        arrays[f"in_{name}_dram"] = a
        args.append(nc.dram_tensor(f"in_{name}_dram", a.shape, _mybir.dt.from_np(a.dtype), kind="ExternalInput").ap())
    for i, (shape, dtype) in enumerate(_OUTS):
        dt = _mybir.dt.from_np(_np.dtype(dtype))
        args.append(nc.dram_tensor(f"out_{i}_dram", shape, dt, kind="ExternalOutput").ap())
    xattn_moe_kernel(nc, *args)
    r = _run(nc, [arrays], core_ids=[0])
    got = tuple(r.results[0][f"out_{i}_dram"] for i in range(len(_OUTS)))
    return got[0]
```
